# Optimizing a Trainium2 kernel written in Bass

```python
import numpy as np
import jax
import jax.numpy as jnp

def _softmax(x, axis=-1):
    return jax.nn.softmax(x, axis=axis)

def _gelu(x):
    return jax.nn.gelu(x, approximate=True)

def _silu(x):
    return jax.nn.silu(x)

def _sigmoid(x):
    return jax.nn.sigmoid(x)

def _layernorm(x, axis=-1, eps=1e-05):
    m = jnp.mean(x, axis=axis, keepdims=True)
    v = jnp.var(x, axis=axis, keepdims=True)
    return (x - m) / jnp.sqrt(v + eps)

def _scatter_add(tgt, idx, src, axis=0):
    return tgt.at[idx].add(src)

def _segment_sum(src, seg, n):
    return jax.ops.segment_sum(src, seg, n)
kernel_name = 'mk_adaln_d1_jaxref_r4_9936e5'

def setup_inputs(seed: int=0):
    np.random.seed(seed)
    _w = jnp.asarray

    def _L0_attn_setup():
        import jax, jax.numpy as jnp
        import numpy as np
        B, T, C = (2, 1024, 256)
        H, M, CHUNK = (16, 64, 128)
        D = C // H
        DELTA = 1e-06
        key = jax.random.key(seed)
        ks = jax.random.split(key, 4)
        x = jax.random.normal(ks[0], (B, T, C), dtype=jnp.float32)
        Wqkv = jax.random.normal(ks[1], (3 * C, C), dtype=jnp.float32) * 0.02
        bqkv = jnp.zeros((3 * C,), dtype=jnp.float32)
        Wout = jax.random.normal(ks[2], (C, C), dtype=jnp.float32) * 0.02
        bout = jnp.zeros((C,), dtype=jnp.float32)
        proj = jax.random.normal(ks[3], (H, D, M), dtype=jnp.float32) / np.sqrt(D)
        return {'x': x, 'Wqkv': Wqkv, 'bqkv': bqkv, 'Wout': Wout, 'bout': bout, 'proj': proj}
    _L0_attn_in = _L0_attn_setup()

    def _L0_ffn_setup():
        import jax, jax.numpy as jnp
        import numpy as np
        D_MODEL = 256
        D_FF = 1024
        NUM_EXPERTS = 8
        B, N = (16, 256)
        key = jax.random.key(seed)
        ks = jax.random.split(key, 7)
        s_in = 1.0 / np.sqrt(D_MODEL)
        s_ff = 1.0 / np.sqrt(D_FF)
        return {'x': jax.random.normal(ks[0], (B, N, D_MODEL), dtype=jnp.float32), 'Wr': jax.random.uniform(ks[1], (D_MODEL, NUM_EXPERTS), jnp.float32, -s_in, s_in), 'br': jax.random.uniform(ks[2], (NUM_EXPERTS,), jnp.float32, -s_in, s_in), 'W1': jax.random.uniform(ks[3], (NUM_EXPERTS, D_MODEL, D_FF), jnp.float32, -s_in, s_in), 'b1': jax.random.uniform(ks[4], (NUM_EXPERTS, D_FF), jnp.float32, -s_in, s_in), 'W2': jax.random.uniform(ks[5], (NUM_EXPERTS, D_FF, D_MODEL), jnp.float32, -s_ff, s_ff), 'b2': jax.random.uniform(ks[6], (NUM_EXPERTS, D_MODEL), jnp.float32, -s_ff, s_ff)}
    _L0_ffn_in = _L0_ffn_setup()
    _L0_c = _w((lambda *s: np.random.randn(*s).astype(np.float32) * 0.05)(8, 256))
    _L0_wmod = _w((lambda *s: np.random.randn(*s).astype(np.float32) * 0.05)(256, 6 * 256) * 256 ** (-0.5))
    _d = {'L0_attn_x': _L0_attn_in['x'], 'L0_attn_Wqkv': _L0_attn_in['Wqkv'], 'L0_attn_bqkv': _L0_attn_in['bqkv'], 'L0_attn_Wout': _L0_attn_in['Wout'], 'L0_attn_bout': _L0_attn_in['bout'], 'L0_attn_proj': _L0_attn_in['proj'], 'L0_ffn_Wr': _L0_ffn_in['Wr'], 'L0_ffn_br': _L0_ffn_in['br'], 'L0_ffn_W1': _L0_ffn_in['W1'], 'L0_ffn_b1': _L0_ffn_in['b1'], 'L0_ffn_W2': _L0_ffn_in['W2'], 'L0_ffn_b2': _L0_ffn_in['b2'], 'L0_c': _L0_c, 'L0_wmod': _L0_wmod}
    _x0 = _d['L0_attn_x']
    _d['L0_attn_x'] = jax.random.normal(jax.random.fold_in(jax.random.key(seed), 1), (8, 1024, 256), dtype=_x0.dtype)
    del _x0
    return _d

def reference(L0_attn_x, L0_attn_Wqkv, L0_attn_bqkv, L0_attn_Wout, L0_attn_bout, L0_attn_proj, L0_ffn_Wr, L0_ffn_br, L0_ffn_W1, L0_ffn_b1, L0_ffn_W2, L0_ffn_b2, L0_c, L0_wmod):

    def _L0_attn_ref(x, Wqkv, bqkv, Wout, bout, proj):
        import jax, jax.numpy as jnp
        import numpy as np
        B, T, C = (2, 1024, 256)
        H, M, CHUNK = (16, 64, 128)
        D = C // H
        DELTA = 1e-06
        b, t, c = x.shape
        qkv = x @ Wqkv.T + bqkv
        q, k, v = jnp.split(qkv, 3, axis=-1)

        def to_heads(z):
            return z.reshape(b, t, H, D).transpose(0, 2, 1, 3).astype(jnp.float32)
        q, k, v = (to_heads(q), to_heads(k), to_heads(v))
        nch = t // CHUNK

        def to_chunks(z):
            return z.reshape(b, H, nch, CHUNK, D).transpose(2, 0, 1, 3, 4)
        qc, kc, vc = (to_chunks(q), to_chunks(k), to_chunks(v))
        mask = jnp.tril(jnp.ones((CHUNK, CHUNK), dtype=jnp.float32))

        def step(carry, inp):
            kv_state, k_state = carry
            q_ch, k_ch, v_ch = inp
            qp = jax.nn.relu(jnp.einsum('bhtd,hdm->bhtm', q_ch, proj))
            kp = jax.nn.relu(jnp.einsum('bhtd,hdm->bhtm', k_ch, proj))
            ctx_hist = jnp.einsum('bhtm,bhmd->bhtd', qp, kv_state)
            norm_hist = jnp.einsum('bhtm,bhm->bht', qp, k_state)
            aw = jnp.einsum('bhtm,bhsm->bhts', qp, kp) * mask
            ctx_intra = jnp.einsum('bhts,bhsd->bhtd', aw, v_ch)
            norm_intra = aw.sum(-1)
            out = (ctx_hist + ctx_intra) / (norm_hist + norm_intra + DELTA)[..., None]
            new_kv = kv_state + jnp.einsum('bhtm,bhtd->bhmd', kp, v_ch)
            new_k = k_state + kp.sum(2)
            return ((new_kv, new_k), out)
        carry0 = (jnp.zeros((b, H, M, D), jnp.float32), jnp.zeros((b, H, M), jnp.float32))
        _, outs = jax.lax.scan(step, carry0, (qc, kc, vc))
        out = outs.transpose(1, 2, 0, 3, 4).reshape(b, H, t, D)
        out = out.transpose(0, 2, 1, 3).reshape(b, t, c)
        return out @ Wout.T + bout

    def _L0_ffn_ref(x, Wr, br, W1, b1, W2, b2):
        import jax, jax.numpy as jnp
        import numpy as np
        D_MODEL = 256
        D_FF = 1024
        NUM_EXPERTS = 8
        B, N = (16, 256)
        scores = jnp.einsum('bh,he->be', x.mean(axis=1), Wr) + br
        top1 = jnp.argmax(scores, axis=-1)
        w1 = W1[top1]
        c1 = b1[top1]
        w2 = W2[top1]
        c2 = b2[top1]
        h = jax.nn.relu(jnp.einsum('bnh,bhf->bnf', x, w1) + c1[:, None, :])
        out = jnp.einsum('bnf,bfh->bnh', h, w2) + c2[:, None, :]
        return out
    x = L0_attn_x
    mod = (_silu(L0_c) @ L0_wmod).reshape(L0_c.shape[0], 6, 1, -1)
    sa, ca, ga, sb, cb, gb = (mod[:, 0], mod[:, 1], mod[:, 2], mod[:, 3], mod[:, 4], mod[:, 5])
    ga = (2 * (ga >= 0) - 1) * jnp.maximum(jnp.abs(ga), 0.25)
    gb = (2 * (gb >= 0) - 1) * jnp.maximum(jnp.abs(gb), 0.25)
    h = _layernorm(x, axis=-1) * (1 + ca) + sa
    x = x + ga * _L0_attn_ref(h, L0_attn_Wqkv, L0_attn_bqkv, L0_attn_Wout, L0_attn_bout, L0_attn_proj)
    h = _layernorm(x, axis=-1) * (1 + cb) + sb
    x = x + gb * _L0_ffn_ref(h, L0_ffn_Wr, L0_ffn_br, L0_ffn_W1, L0_ffn_b1, L0_ffn_W2, L0_ffn_b2)
    return x

_drawn_inputs = setup_inputs


def setup_inputs(seed=0):
    import zlib

    import numpy as np

    out = dict(_drawn_inputs(seed))
    spreads = {'L0_attn_bqkv': (0.0, 0.8), 'L0_attn_bout': (0.0, 0.1)}
    factors = {'L0_attn_Wqkv': 2.695, 'L0_attn_proj': 21.688, 'L0_ffn_b1': 8.0, 'L0_ffn_b2': 8.0}
    for name, (base, spread) in spreads.items():
        noise = np.random.default_rng([zlib.crc32(name.encode()), seed]).standard_normal(out[name].shape)
        drawn = base * np.exp(spread * noise) if base else spread * noise
        out[name] = jnp.asarray(drawn.astype(out[name].dtype))
    for name, factor in factors.items():
        out[name] = (out[name] * factor).astype(out[name].dtype)
    return out
```

```python
from contextlib import ExitStack

import concourse.bass as bass
from concourse import mybir

F32 = mybir.dt.float32
F32R = mybir.dt.float32r
U32 = mybir.dt.uint32
ALU = mybir.AluOpType
ACT = mybir.ActivationFunctionType

P = 128
B, T, C = 8, 1024, 256
H, D, M = 16, 16, 64
E, F = 8, 1024
NPAIR = H // 2
CJ = C // P
FC = F // P
DUO = 2 * P
DPB = T // DUO
ND = B * DPB
VW = D + 1
EPS = 1e-5
DELTA = 1e-6
FFN_LAG = 4
LOOP = range(9, 13)
TURNS = 5


class Step:

    def __init__(self, n, k=None):
        self.n, self.k = n, k

    def at(self, f):
        a = f(self.n)
        if self.k is None:
            return a
        slope = f(self.n + DPB) - a
        if slope == 0:
            return a
        assert f(self.n + 2 * DPB) - a == 2 * slope
        return self.k * slope + a


def has_front(n):
    return n + 1 < ND


def has_attn(n):
    return 0 <= n < ND


def has_ln2(n):
    return 1 <= n <= ND


def has_up(n):
    return FFN_LAG <= n < ND + FFN_LAG


def has_down(n):
    return FFN_LAG + 1 <= n < ND + FFN_LAG + 1


def has_route(n):
    return n % DPB == 0 and DPB <= n <= ND


def is_last(n, i):
    return n % DPB == DPB - 1 and i == 1


def act_fills(n):
    out = []
    if has_front(n):
        out += ["xT"]
    if has_attn(n):
        out += ["kp00", "kp01"]
    if has_ln2(n):
        out += ["x2T"]
    if has_front(n):
        out += ["qk0", "qk1"] + [f"feat0{j}" for j in range(4)]
    if has_attn(n) and not is_last(n, 1):
        out += ["kp10", "kp11"]
    if has_front(n):
        out += [f"feat1{j}" for j in range(4)]
    if has_up(n):
        out += [f"up{q}" for q in range(4)]
    return out


def dve_fills(n):
    out = []
    if has_down(n):
        out += ["down0"]
    if has_route(n):
        out += ["route"]
    if has_front(n):
        out += ["v"]
    if has_down(n):
        out += ["down1"]
    if has_attn(n):
        out += ["aT0", "o0", "aT1", "o1"]
    return out


def fill(fills, name):
    return lambda n: sum(len(fills(m)) for m in range(-1, n)) + fills(n).index(name)


def chunks_with_state(n, i):
    return (n // DPB) * (2 * DPB - 1) + 2 * (n % DPB) + i + 1


def program(nc, x, wqkv, bqkv, wout, bout, proj, wr, br, w1, b1, w2, b2, c, wmod, out):
    with ExitStack() as ctx:
        ctx.enter_context(nc.allow_non_contiguous_dma(reason="small bias and condition loads"))

        def sb(name, shape, dt=F32):
            return ctx.enter_context(nc.sbuf_tensor(name, shape, dt))

        def pb(name):
            return ctx.enter_context(nc.psum_tensor(name, [P, 512], F32))

        def sem(name):
            return ctx.enter_context(nc.semaphore(name))

        ident = sb("ident", [P, P])
        mask = sb("mask", [P, P])
        wqkvT_hi = sb("wqkvT_hi", [P, CJ, 3 * C], F32R)
        wqkvT_lo = sb("wqkvT_lo", [P, CJ, 3 * C], F32R)
        woT = sb("woT", [P, CJ, C])
        wog = sb("wog", [P, CJ, C])
        wog_hi = sb("wog_hi", [P, CJ, C], F32R)
        wog_lo = sb("wog_lo", [P, CJ, C], F32R)
        pbd = sb("pbd", [P, CJ, P])
        pbd_hi = sb("pbd_hi", [P, CJ, P], F32R)
        pbd_lo = sb("pbd_lo", [P, CJ, P], F32R)
        bqk = sb("bqk", [P, 4])
        bv = sb("bv", [P, C])
        bo = sb("bo", [P, C])
        gbo = sb("gbo", [P, C])
        wr_sb = sb("wr_sb", [P, CJ, E])
        br_sb = sb("br_sb", [1, E])
        cT = sb("cT", [P, CJ, B])
        scT = sb("scT", [P, CJ, B])
        modT = sb("modT", [P, 4, CJ, B])
        ga = sb("ga", [P, C])
        gb = sb("gb", [P, C])

        xin = sb("xin", [P, DPB, 2, C])
        x1 = sb("x1", [P, DPB, 2, C])
        res = sb("res", [P, 2, 2, C])
        eps = sb("eps", [P, 1])
        stats = [sb(f"stats{q}", [P, 2, 6]) for q in range(2)]
        mv = [sb(f"mv{q}", [P, 2, 2]) for q in range(2)]
        std = [sb(f"std{q}", [P, 2]) for q in range(2)]
        rstd = [sb(f"rstd{q}", [P, 2]) for q in range(2)]
        xn = sb("xn", [P, 2, C])
        xn2 = sb("xn2", [P, 2, C])
        hT = sb("hT", [P, CJ, DUO])
        hT_hi = sb("hT_hi", [P, CJ, DUO], F32R)
        hT_lo = sb("hT_lo", [P, CJ, DUO], F32R)
        hF = sb("hF", [P, CJ, DUO])
        hF_hi = sb("hF_hi", [P, DPB, CJ, DUO], F32R)
        hF_lo = sb("hF_lo", [P, DPB, CJ, DUO], F32R)
        hsum = sb("hsum", [P, CJ, DPB])
        qkT = sb("qkT", [P, 2, CJ, DUO])
        qkT_hi = sb("qkT_hi", [P, 2, CJ, DUO], F32R)
        qkT_lo = sb("qkT_lo", [P, 2, CJ, DUO], F32R)
        feat = [[sb(f"feat{r}{w}", [P, NPAIR, DUO]) for w in "qk"] for r in range(2)]
        kp = sb("kp", [P, NPAIR, P])
        vaug = sb("vaug", [P, 2, 2, H, VW])
        awT = sb("awT", [P, 2, 2, 4, P])
        kvbd = sb("kvbd", [P, NPAIR, 2 * VW])
        den = sb("den", [P, H])
        rden = sb("rden", [P, H])
        attn = sb("attn", [P, C])
        aT_hi = sb("aT_hi", [P, CJ, P], F32R)
        aT_lo = sb("aT_lo", [P, CJ, P], F32R)

        w1raw = sb("w1raw", [P, CJ, F])
        w1_hi = sb("w1_hi", [P, CJ, FC, P], F32R)
        w1_lo = sb("w1_lo", [P, CJ, FC, P], F32R)
        w2raw = w1raw[:, :, :].rearrange("p j f -> p (j f)").rearrange("p (f c) -> p f c", c=C)
        w2_hi = sb("w2_hi", [P, FC, C], F32R)
        w2_lo = sb("w2_lo", [P, FC, C], F32R)
        b1_sb = sb("b1_sb", [P, FC])
        b2_sb = sb("b2_sb", [P, C])
        gb2 = sb("gb2", [P, C])
        h1 = sb("h1", [P, 2, 2, DUO])
        h1_hi = sb("h1_hi", [P, FC, DUO], F32R)
        h1_lo = sb("h1_lo", [P, FC, DUO], F32R)
        score = sb("score", [1, E])
        best = sb("best", [1, E])
        which = sb("which", [1, E], U32)

        wqkv_raw = feat[0][0][:, :, :].rearrange("p a t -> p (a t)")[:, 0:6 * C].rearrange("p (o c) -> p o c", c=C)
        wout_raw = feat[0][1][:, :, :].rearrange("p a t -> p (a t)")[:, 0:2 * C].rearrange("p (o c) -> p o c", c=C)
        wmod_a = w1raw[:, :, :]
        wmod_b = feat[1][0][:, 0:4, :].rearrange("p a t -> p (a t)").rearrange("p (j n) -> p j n", j=CJ)
        gate_raw, gate_abs, gate_row = (feat[1][1][0:B, 2 * q:2 * q + 2, :] for q in range(3))

        gates_dram = nc.dram_tensor("gates_dram", (B, 2, C), F32, kind="Internal").ap()

        act_bank = [pb("act_bank0"), pb("act_bank1")]
        dve_bank = [pb("dve_bank0"), pb("dve_bank1")]
        aw_bank = [pb("aw_even"), pb("aw_odd")]
        ctx_bank = pb("ctx_bank")
        kv_bank = pb("kv_bank")

        s_wqkv, s_wout, s_wmod, s_small, s_pbd = sem("s_wqkv"), sem("s_wout"), sem("s_wmod"), sem("s_small"), sem("s_pbd")
        zeroed, consts_ready = sem("zeroed"), sem("consts_ready")
        silu_ready = sem("silu_ready")
        setup_filled, setup_freed = sem("setup_filled"), sem("setup_freed")
        mod_filled, mod_ready = sem("mod_filled"), sem("mod_ready")
        gate_chain, gates_stored = sem("gate_chain"), sem("gates_stored")
        pbd_ready = sem("pbd_ready")
        x_loaded = sem("x_loaded")
        ga_loaded, gb_loaded = sem("ga_loaded"), sem("gb_loaded")
        w1_loaded, w2_loaded, b1_loaded, b2_loaded = sem("w1_loaded"), sem("w2_loaded"), sem("b1_loaded"), sem("b2_loaded")
        out_stored = sem("out_stored")
        act_filled, act_freed = sem("act_filled"), sem("act_freed")
        dve_filled, dve_freed = sem("dve_filled"), sem("dve_freed")
        aw_filled, aw_ready = sem("aw_filled"), sem("aw_ready")
        ctx_filled, attn_ready = sem("ctx_filled"), sem("attn_ready")
        kv_filled, kv_ready = sem("kv_filled"), sem("kv_ready")
        stats_chain = [sem("stats_chain0"), sem("stats_chain1")]
        std_ready = [sem("std_ready0"), sem("std_ready1")]
        rstd_ready = [sem("rstd_ready0"), sem("rstd_ready1")]
        xn_ready, xn2_ready = sem("xn_ready"), sem("xn2_ready")
        hT_split, hF_split, qk_split = sem("hT_split"), sem("hF_split"), sem("qk_split")
        norm_chain, aT_hi_ready = sem("norm_chain"), sem("aT_hi_ready")
        wo_chain, wo_split = sem("wo_chain"), sem("wo_split")
        xb_ready, res_copied, x2_ready = sem("xb_ready"), sem("res_copied"), sem("x2_ready")
        score_chain, expert_ready = sem("score_chain"), sem("expert_ready")
        w1_hi_ready, w1_split, w2_chain, w2_split = sem("w1_hi_ready"), sem("w1_split"), sem("w2_chain"), sem("w2_split")
        h1_split = sem("h1_split")

        x_v = x.rearrange("b (d i p) c -> p (b d) i c", i=2, p=P)
        out_v = out.rearrange("b (d i p) c -> p (b d) i c", i=2, p=P)
        gates_v = gates_dram.rearrange("b g c -> g b c")

        block = ctx.enter_context(nc.Block())

        def run(eng, step):
            for n in range(-1, LOOP[0]):
                step(Step(n))
            with eng.Fori(0, TURNS) as k:
                for n in LOOP:
                    step(Step(n, k))
            for n in range(LOOP[0] + DPB * TURNS, ND + FFN_LAG + 1):
                step(Step(n))

        def wait_apart(eng, of, count):
            count = eng.to_reg(count) if not isinstance(count, int) else count
            eng.wait_ge(consts_ready, 1)
            eng.wait_ge(of, count)

        @block.sync
        def _(sp):
            sp.dma_start(wqkv_raw, wqkv.rearrange("(o p) c -> p o c", p=P)).then_inc(s_wqkv, 16)
            sp.dma_start(xin[:, 0, :, :], x_v[:, 0, :, :]).then_inc(x_loaded, 16)
            sp.dma_start(wout_raw, wout.rearrange("(o p) c -> p o c", p=P)).then_inc(s_wout, 16)
            for m in (1, 2):
                sp.wait_ge(x_loaded, 16 * m)
                sp.dma_start(xin[:, m, :, :], x_v[:, m, :, :]).then_inc(x_loaded, 16)
            sp.wait_ge(gate_chain, 3)
            sp.dma_start(gates_dram, gate_row[:, :, :]).then_inc(gates_stored, 16)
            sp.wait_ge(gates_stored, 16)
            sp.dma_start(ga[:, :], gates_v[0, 0:1, :].to_broadcast([P, C])).then_inc(ga_loaded, 16)

            def step(s):
                n = s.n
                if 0 <= n and n + 3 < ND:
                    if n >= 1:
                        wait_apart(sp, xn2_ready, s.at(lambda n: 2 * n))
                    wait_apart(sp, x_loaded, s.at(lambda n: 16 * (n + 3)))
                    sp.dma_start(xin[:, (n + 3) % DPB, :, :],
                                 x_v[:, bass.ds(s.at(lambda n: n + 3), 1), :, :].rearrange("p m i c -> p (m i) c"))\
                      .then_inc(x_loaded, 16)
                if has_route(n):
                    wait_apart(sp, expert_ready, s.at(lambda n: n // DPB))
                    expert = sp.value_load(which[0:1, 0:1], min_val=0, max_val=E - 1)
                    if n > DPB:
                        wait_apart(sp, w2_split, s.at(lambda n: n // DPB - 1))
                        wait_apart(sp, h1_split, s.at(lambda n: 4 * (n - FFN_LAG)))
                    sp.dma_start(w1raw[:, :, :], w1[bass.ds(expert, 1), :, :].rearrange("e (j p) f -> p (e j) f", p=P))\
                      .then_inc(w1_loaded, 16)
                    sp.dma_start(b1_sb[:, :], b1[bass.ds(expert, 1), :].rearrange("e (p f) -> p (e f)", p=P))\
                      .then_inc(b1_loaded, 16)
                    wait_apart(sp, w1_split, s.at(lambda n: n // DPB))
                    sp.dma_start(w2raw[:, :, :], w2[bass.ds(expert, 1), :, :].rearrange("e (p f) c -> p (e f) c", p=P))\
                      .then_inc(w2_loaded, 16)
                    sp.dma_start(b2_sb[:, :], b2[bass.ds(expert, 1), :].to_broadcast([P, C])).then_inc(b2_loaded, 16)
                    sp.dma_start(gb[:, :], gates_v[1, bass.ds(s.at(lambda n: n // DPB - 1), 1), :].to_broadcast([P, C]))\
                      .then_inc(gb_loaded, 16)
                if has_down(n):
                    if n > FFN_LAG + 1:
                        wait_apart(sp, out_stored, s.at(lambda n: 16 * (n - FFN_LAG - 1)))
                    wait_apart(sp, dve_freed, s.at(lambda n: fill(dve_fills, "down1")(n) + 1))
                    sp.dma_start(out_v[:, bass.ds(s.at(lambda n: n - FFN_LAG - 1), 1), :, :]
                                 .rearrange("p m i c -> p (m i) c"), res[:, (n - FFN_LAG - 1) % 2, :, :])\
                      .then_inc(out_stored, 16)
                if n % DPB == 1 and n < ND - DPB:
                    wait_apart(sp, wo_split, s.at(lambda n: n // DPB + 1))
                    sp.dma_start(ga[:, :], gates_v[0, bass.ds(s.at(lambda n: n // DPB + 1), 1), :].to_broadcast([P, C]))\
                      .then_inc(ga_loaded, 16)

            run(sp, step)
            sp.wait_ge(out_stored, 16 * ND)

        @block.scalar
        def _(act):
            for j in range(CJ):
                act.dma_start(cT[:, j, :], c[:, j * P:(j + 1) * P].rearrange("b p -> p b")).then_inc(s_small, 16)
            act.dma_start(wmod_a, wmod.rearrange("(j p) n -> p j n", p=P)[:, :, 0:1024]).then_inc(s_wmod, 16)
            act.dma_start(wmod_b, wmod.rearrange("(j p) n -> p j n", p=P)[:, :, 1024:1536]).then_inc(s_wmod, 16)
            act.dma_start(wr_sb[:, :, :], wr.rearrange("(j p) e -> p j e", p=P)).then_inc(s_small, 16)
            act.dma_start(br_sb[:, :], br.rearrange("(a e) -> a e", a=1)).then_inc(s_small, 16)
            act.dma_start(bqk[:, :], bqkv[0:2 * C].rearrange("(o p) -> p o", p=P)).then_inc(s_small, 16)
            act.dma_start(bv[:, :], bqkv[2 * C:3 * C].rearrange("(a c) -> a c", a=1).to_broadcast([P, C])).then_inc(s_small, 16)
            act.dma_start(bo[:, :], bout.rearrange("(a c) -> a c", a=1).to_broadcast([P, C])).then_inc(s_small, 16)
            act.wait_ge(zeroed, 1)
            for h in range(H):
                act.dma_start(pbd[(h % 8) * D:(h % 8 + 1) * D, h // 8, (h % 2) * M:(h % 2 + 1) * M], proj[h, :, :])\
                   .then_inc(s_pbd, 16)
            act.wait_ge(s_small, 16 * 7)
            nc.scalar.activation(scT[:, :, :], cT[:, :, :], ACT.Silu).then_inc(silu_ready, 1)

            def drain(s, name):
                if name in ("xT", "x2T"):
                    wait_apart(act, act_filled, s.at(lambda n: fill(act_fills, name)(n) + 1))
                else:
                    act.wait_ge(act_filled, s.at(lambda n: fill(act_fills, name)(n) + 1))
                return act_bank[fill(act_fills, name)(s.n) % 2]

            def kp_copy(s, i):
                for half in range(2):
                    ps = drain(s, f"kp{i}{half}")
                    nc.scalar.activation(kp[:, 4 * half:4 * half + 4, :], ps[:, :].rearrange("p (a s) -> p a s", s=P),
                                         ACT.Copy).then_inc(act_freed, 1)

            def modulate(s, ps, full, hi, shift, gain, batch, sums):
                for j in range(CJ):
                    src = ps[:, j * DUO:(j + 1) * DUO]
                    scale = modT[:, gain, j, bass.ds(batch, 1)]
                    bias = modT[:, shift, j, bass.ds(batch, 1)]
                    nc.scalar.activation(full[:, j, :], src, ACT.Identity, bias=bias, scale=scale,
                                         accum_out=None if sums is None else sums[:, j:j + 1])
                    last = nc.scalar.activation(hi[:, j, :], src, ACT.Identity, bias=bias, scale=scale)
                return last

            def state_copy(s, i):
                act.wait_ge(kv_filled, s.at(lambda n: chunks_with_state(n, i)))
                ps = kv_bank[:, 0:NPAIR * 2 * VW].rearrange("p (a w) -> p a w", w=2 * VW)
                nc.scalar.activation(kvbd[0:M, :, 0:VW], ps[0:M, :, 0:VW], ACT.Copy)
                nc.scalar.activation(kvbd[M:P, :, VW:2 * VW], ps[M:P, :, VW:2 * VW], ACT.Copy).then_inc(kv_ready, 1)

            def features(s, w):
                dst = feat[(s.n + 1) % 2][w][:, :, :].rearrange("p (g j) t -> p g j t", j=4)
                for j in range(4):
                    ps = drain(s, f"feat{w}{j}")
                    nc.scalar.activation(dst[:, :, j, :], ps[:, :].rearrange("p (g t) -> p g t", t=DUO), ACT.Relu)\
                      .then_inc(act_freed, 1)

            def deviation(s, q, duo):
                act.wait_ge(stats_chain[q], s.at(lambda n: 4 * duo(n) + 4))
                nc.scalar.activation(std[q][:, :], mv[q][:, :, 1], ACT.Sqrt, bias=eps[:, :]).then_inc(std_ready[q], 1)

            def step(s):
                n = s.n
                if n == -1:
                    act.wait_ge(zeroed, 6)
                    deviation(Step(-2), 0, lambda n: n + 2)
                if has_front(n):
                    ps = drain(s, "xT")
                    if n >= 0:
                        wait_apart(act, hT_split, s.at(lambda n: n + 1))
                    modulate(s, ps, hT, hT_hi, 0, 1, s.at(lambda n: (n + 1) // DPB), None).then_inc(act_freed, 1)
                if has_ln2(n):
                    deviation(s, 1, lambda n: n - 1)
                if has_attn(n):
                    kp_copy(s, 0)
                if has_ln2(n):
                    ps = drain(s, "x2T")
                    if n >= 2:
                        wait_apart(act, hF_split, s.at(lambda n: n - 1))
                    slot = (n - 1) % DPB
                    modulate(s, ps, hF, hF_hi[:, slot, :, :], 2, 3, s.at(lambda n: (n - 1) // DPB),
                             hsum[:, :, slot]).then_inc(act_freed, 1)
                if has_front(n):
                    for w in range(2):
                        ps = drain(s, f"qk{w}")
                        if n >= 0:
                            act.wait_ge(qk_split, s.at(lambda n: 2 * (n + 1)))
                        for g in range(CJ):
                            src = ps[:, g * DUO:(g + 1) * DUO]
                            bias = bqk[:, 2 * w + g:2 * w + g + 1]
                            nc.scalar.activation(qkT[:, w, g, :], src, ACT.Identity, bias=bias)
                            last = nc.scalar.activation(qkT_hi[:, w, g, :], src, ACT.Identity, bias=bias)
                        last.then_inc(act_freed, 1)
                if has_attn(n):
                    state_copy(s, 0)
                if has_front(n):
                    features(s, 0)
                if n + 2 < ND:
                    deviation(s, 0, lambda n: n + 2)
                if has_attn(n) and not is_last(n, 1):
                    kp_copy(s, 1)
                if has_front(n):
                    features(s, 1)
                if has_attn(n) and not is_last(n, 1):
                    state_copy(s, 1)
                if has_up(n):
                    if n % DPB == 0:
                        act.wait_ge(b1_loaded, s.at(lambda n: 16 * (n // DPB)))
                    for q in range(4):
                        ps = drain(s, f"up{q}")
                        if n > FFN_LAG or q >= 2:
                            act.wait_ge(h1_split, s.at(lambda n: 4 * (n - FFN_LAG) + q - 1))
                        for a in range(2):
                            src = ps[:, a * DUO:(a + 1) * DUO]
                            bias = b1_sb[:, 2 * q + a:2 * q + a + 1]
                            nc.scalar.activation(h1[:, q % 2, a, :], src, ACT.Relu, bias=bias)
                            last = nc.scalar.activation(h1_hi[:, 2 * q + a, :], src, ACT.Relu, bias=bias)
                        last.then_inc(act_freed, 1)

            run(act, step)

        @block.gpsimd
        def _(pool):
            nc.gpsimd.memset(pbd[:, :, :], 0.0).then_inc(zeroed, 1)
            nc.gpsimd.memset(ident[:, :], 0.0).then_inc(zeroed, 1)
            nc.gpsimd.memset(mask[:, :], 1.0).then_inc(zeroed, 1)
            nc.gpsimd.memset(vaug[:, :, :, :, D:VW], 1.0).then_inc(zeroed, 1)
            nc.gpsimd.memset(kvbd[:, :, :], 0.0).then_inc(zeroed, 1)
            nc.gpsimd.memset(eps[:, :], EPS).then_inc(zeroed, 1)
            pool.wait_ge(zeroed, 6)
            nc.gpsimd.affine_select(out=ident[:, :], in_=ident[:, :], compare_op=ALU.not_equal, fill=1.0, base=0,
                                    pattern=[[-1, P]], channel_multiplier=1).then_inc(consts_ready, 1)
            nc.gpsimd.affine_select(out=mask[:, :], in_=mask[:, :], compare_op=ALU.is_ge, fill=0.0, base=0,
                                    pattern=[[1, P]], channel_multiplier=-1).then_inc(consts_ready, 1)

            def minus_hi(lo, full, hi):
                return nc.gpsimd.tensor_tensor(lo, full, hi.bitcast(F32), ALU.subtract)

            def step(s):
                n = s.n
                if has_front(n):
                    pool.wait_ge(act_freed, s.at(lambda n: fill(act_fills, "xT")(n) + 1))
                    minus_hi(hT_lo[:, :, :], hT[:, :, :], hT_hi[:, :, :]).then_inc(hT_split, 1)
                if has_attn(n) and n % DPB == 0:
                    pool.wait_ge(ga_loaded, s.at(lambda n: 16 * (n // DPB + 1)))
                    if n == 0:
                        pool.wait_ge(setup_freed, 4)
                        pool.wait_ge(s_small, 16 * 7)
                    else:
                        pool.wait_ge(xn2_ready, s.at(lambda n: 2 * n))
                    nc.gpsimd.tensor_tensor(gbo[:, :], bo[:, :], ga[:, :], ALU.mult).then_inc(wo_chain, 1)
                    for j in range(CJ):
                        nc.gpsimd.tensor_tensor(wog[:, j, :], woT[:, j, :], ga[:, :], ALU.mult).then_inc(wo_chain, 1)
                    wait_apart(pool, wo_chain, s.at(lambda n: 4 * (n // DPB) + 3))
                    nc.gpsimd.tensor_copy(wog_hi[:, :, :], wog[:, :, :]).then_inc(wo_chain, 1)
                    pool.wait_ge(wo_chain, s.at(lambda n: 4 * (n // DPB) + 4))
                    minus_hi(wog_lo[:, :, :], wog[:, :, :], wog_hi[:, :, :]).then_inc(wo_split, 1)
                if has_down(n):
                    slot = (n - FFN_LAG - 1) % 2
                    pool.wait_ge(res_copied, s.at(lambda n: n - FFN_LAG))
                    for i in range(2):
                        nc.gpsimd.tensor_tensor(res[:, slot, i, :], res[:, slot, i, :], gb2[:, :], ALU.add)\
                          .then_inc(x2_ready, 1)
                if has_ln2(n):
                    pool.wait_ge(act_freed, s.at(lambda n: fill(act_fills, "x2T")(n) + 1))
                    slot = (n - 1) % DPB
                    minus_hi(hF_lo[:, slot, :, :], hF[:, :, :], hF_hi[:, slot, :, :]).then_inc(hF_split, 1)
                if has_attn(n):
                    pool.wait_ge(xn_ready, s.at(lambda n: 2 * (n + 1)))
                    for i in range(2):
                        nc.gpsimd.tensor_tensor(xin[:, n % DPB, i, :], xin[:, n % DPB, i, :], gbo[:, :], ALU.add)\
                          .then_inc(xb_ready, 1)
                if has_up(n):
                    wait_apart(pool, xn2_ready, s.at(lambda n: 2 * (n - FFN_LAG + 1)))
                    if n >= FFN_LAG + 2:
                        wait_apart(pool, out_stored, s.at(lambda n: 16 * (n - FFN_LAG - 1)))
                    nc.gpsimd.tensor_copy(res[:, (n - FFN_LAG) % 2, :, :], x1[:, (n - FFN_LAG) % DPB, :, :])\
                      .then_inc(res_copied, 1)
                if has_front(n):
                    for w in range(2):
                        pool.wait_ge(act_freed, s.at(lambda n: fill(act_fills, f"qk{w}")(n) + 1))
                        minus_hi(qkT_lo[:, w, :, :], qkT[:, w, :, :], qkT_hi[:, w, :, :]).then_inc(qk_split, 1)
                if has_route(n):
                    wait_apart(pool, w1_loaded, s.at(lambda n: 16 * (n // DPB)))
                    for j in range(CJ):
                        src = w1raw[:, j, :].rearrange("p (q f) -> p f q", f=FC)
                        nc.gpsimd.tensor_copy(w1_hi[:, j, :, :], src).then_inc(w1_hi_ready, 1)
                    for j in range(CJ):
                        src = w1raw[:, j, :].rearrange("p (q f) -> p f q", f=FC)
                        pool.wait_ge(w1_hi_ready, s.at(lambda n: 2 * (n // DPB - 1) + j + 1))
                        last = minus_hi(w1_lo[:, j, :, :], src, w1_hi[:, j, :, :])
                    last.then_inc(w1_split, 1)
                    pool.wait_ge(w2_loaded, s.at(lambda n: 16 * (n // DPB)))
                    pool.wait_ge(gb_loaded, s.at(lambda n: 16 * (n // DPB)))
                    pool.wait_ge(b2_loaded, s.at(lambda n: 16 * (n // DPB)))
                    if n > DPB:
                        pool.wait_ge(dve_freed, s.at(lambda n: fill(dve_fills, "down1")(n) + 1))
                    for f in range(FC):
                        nc.gpsimd.tensor_tensor(w2raw[:, f, :], w2raw[:, f, :], gb[:, :], ALU.mult).then_inc(w2_chain, 1)
                    nc.gpsimd.tensor_tensor(gb2[:, :], b2_sb[:, :], gb[:, :], ALU.mult).then_inc(w2_chain, 1)
                    wait_apart(pool, w2_chain, s.at(lambda n: (FC + 2) * (n // DPB) - 1))
                    nc.gpsimd.tensor_copy(w2_hi[:, :, :], w2raw[:, :, :]).then_inc(w2_chain, 1)
                    pool.wait_ge(w2_chain, s.at(lambda n: (FC + 2) * (n // DPB)))
                    minus_hi(w2_lo[:, :, :], w2raw[:, :, :], w2_hi[:, :, :]).then_inc(w2_split, 1)
                if has_up(n):
                    for q in range(4):
                        pool.wait_ge(act_freed, s.at(lambda n: fill(act_fills, f"up{q}")(n) + 1))
                        minus_hi(h1_lo[:, 2 * q:2 * q + 2, :], h1[:, q % 2, :, :], h1_hi[:, 2 * q:2 * q + 2, :])\
                          .then_inc(h1_split, 1)

            run(pool, step)

        @block.vector
        def _(dve):
            for f in range(4):
                dve.wait_ge(setup_filled, f + 1)
                ps = dve_bank[f % 2]
                if f < 3:
                    dst = slice(f * C, (f + 1) * C)
                    src = ps[:, :].rearrange("p (j o) -> p j o", j=CJ)
                    nc.vector.tensor_copy(wqkvT_hi[:, :, dst], src).then_inc(pbd_ready, 1)
                    dve.wait_ge(pbd_ready, f + 1)
                    nc.vector.tensor_tensor(wqkvT_lo[:, :, dst], src, wqkvT_hi[:, :, dst].bitcast(F32), ALU.subtract)\
                      .then_inc(setup_freed, 1)
                else:
                    nc.vector.tensor_copy(woT[:, :, :], ps[:, :].rearrange("p (j o) -> p j o", j=CJ)).then_inc(setup_freed, 1)
            dve.wait_ge(s_pbd, 16 * H)
            nc.vector.tensor_copy(pbd_hi[:, :, :], pbd[:, :, :]).then_inc(pbd_ready, 1)
            dve.wait_ge(pbd_ready, 4)
            nc.vector.tensor_tensor(pbd_lo[:, :, :], pbd[:, :, :], pbd_hi[:, :, :].bitcast(F32), ALU.subtract)\
              .then_inc(pbd_ready, 1)
            dve.wait_ge(mod_filled, 1)
            ps = ctx_bank[:, 0:4 * CJ * B].rearrange("p (q j b) -> p q j b", q=4, j=CJ)
            for q in range(4):
                nc.vector.tensor_scalar(modT[:, q, :, :], ps[:, q, :, :], float(q % 2), None, ALU.add).then_inc(mod_ready, 1)
            dve.wait_ge(mod_filled, 2)
            nc.vector.tensor_copy(gate_raw[:, :, :], kv_bank[0:B, :].rearrange("p (q c) -> p q c", q=2)).then_inc(gate_chain, 1)
            dve.wait_ge(gate_chain, 1)
            nc.vector.scalar_tensor_tensor(gate_abs, gate_raw, -1.0, gate_raw, ALU.mult, ALU.max).then_inc(mod_ready, 1)
            dve.wait_ge(mod_ready, 5)
            nc.vector.tensor_scalar(gate_abs, gate_abs, 0.25, None, ALU.max).then_inc(mod_ready, 1)
            nc.vector.tensor_scalar(gate_row[:, :, :], gate_raw[:, :, :], 0.0, 2.0, ALU.is_ge, ALU.mult).then_inc(gate_chain, 1)
            dve.wait_ge(mod_ready, 6)
            dve.wait_ge(gate_chain, 2)
            nc.vector.scalar_tensor_tensor(gate_row[:, :, :], gate_row[:, :, :], -1.0, gate_abs[:, :, :],
                                           ALU.add, ALU.mult).then_inc(gate_chain, 1)

            def drain(s, name):
                dve.wait_ge(dve_filled, s.at(lambda n: fill(dve_fills, name)(n) + 1))
                return dve_bank[fill(dve_fills, name)(s.n) % 2]

            def measure(s, q, i, src, duo):
                nc.vector.bn_stats(stats[q][:, i, :], src).then_inc(stats_chain[q], 1)
                wait_apart(dve, stats_chain[q], s.at(lambda n: 4 * duo(n) + 2 * i + 1))
                nc.vector.bn_aggr(mv[q][:, i, :], stats[q][:, i, :]).then_inc(stats_chain[q], 1)

            def apply_norm(s, q, src, dst, duo, done):
                dve.wait_ge(std_ready[q], s.at(lambda n: duo(n) + 1))
                nc.vector.reciprocal(rstd[q][:, :], std[q][:, :]).then_inc(rstd_ready[q], 1)
                dve.wait_ge(rstd_ready[q], s.at(lambda n: duo(n) + 1))
                for i in range(2):
                    nc.vector.tensor_scalar(dst[:, i, :], src[:, i, :], mv[q][:, i, 0:1], rstd[q][:, i:i + 1],
                                            ALU.subtract, ALU.mult).then_inc(done, 1)

            def measure_first(s):
                dve.wait_ge(x_loaded, s.at(lambda n: 16 * (n + 3)))
                for i in range(2):
                    measure(s, 0, i, xin[:, (s.n + 2) % DPB, i, :], lambda n: n + 2)

            def apply_first(s):
                if s.n >= -1:
                    dve.wait_ge(act_filled, s.at(lambda n: fill(act_fills, "xT")(n) + 1))
                apply_norm(s, 0, xin[:, (s.n + 2) % DPB, :, :], xn, lambda n: n + 2, xn_ready)

            def mask_weights(s, i):
                for r in range(2):
                    for a in range(2):
                        dve.wait_ge(aw_filled, s.at(lambda n: 4 * (2 * n + i) + 2 * r + a + 1))
                        nc.vector.tensor_tensor(awT[:, r, a, :, :], aw_bank[a][:, :].rearrange("p (j t) -> p j t", t=P),
                                                mask[:, :].rearrange("p (a t) -> p a t", a=1).to_broadcast([P, 4, P]),
                                                ALU.mult).then_inc(aw_ready, 1)

            def normalise(s, i):
                dve.wait_ge(ctx_filled, s.at(lambda n: 2 * n + i + 1))
                ps = ctx_bank[:, 0:H * VW].rearrange("p (h w) -> p h w", w=VW)
                nc.vector.tensor_scalar(den[:, :], ps[:, :, D], DELTA, None, ALU.add).then_inc(norm_chain, 1)
                dve.wait_ge(norm_chain, s.at(lambda n: 2 * (2 * n + i) + 1))
                nc.vector.reciprocal(rden[:, :], den[:, :]).then_inc(norm_chain, 1)
                dve.wait_ge(norm_chain, s.at(lambda n: 2 * (2 * n + i) + 2))
                nc.vector.tensor_tensor(attn[:, :].rearrange("p (h d) -> p h d", d=D), ps[:, :, 0:D],
                                        rden[:, :].rearrange("p (h a) -> p h a", a=1).to_broadcast([P, H, D]),
                                        ALU.mult).then_inc(attn_ready, 1)

            def split_attn(s, i):
                ps = drain(s, f"aT{i}")
                src = ps[:, 0:C].rearrange("p (j t) -> p j t", t=P)
                nc.vector.tensor_copy(aT_hi[:, :, :], src).then_inc(aT_hi_ready, 1)
                dve.wait_ge(aT_hi_ready, s.at(lambda n: 2 * n + i + 1))
                nc.vector.tensor_tensor(aT_lo[:, :, :], src, aT_hi[:, :, :].bitcast(F32), ALU.subtract).then_inc(dve_freed, 1)

            def residual(s, i):
                ps = drain(s, f"o{i}")
                slot = s.n % DPB
                dve.wait_ge(xb_ready, s.at(lambda n: 2 * n + i + 1))
                if has_up(s.n) and i == 0:
                    dve.wait_ge(res_copied, s.at(lambda n: n - FFN_LAG + 1))
                nc.vector.tensor_tensor(x1[:, slot, i, :], ps[:, 0:C], xin[:, slot, i, :], ALU.add).then_inc(dve_freed, 1)
                dve.wait_ge(dve_freed, s.at(lambda n: fill(dve_fills, f"o{i}")(n) + 1))
                measure(s, 1, i, x1[:, slot, i, :], lambda n: n)

            def finish(s, i):
                ps = drain(s, f"down{i}")
                slot = (s.n - FFN_LAG - 1) % 2
                dve.wait_ge(x2_ready, s.at(lambda n: 2 * (n - FFN_LAG - 1) + i + 1))
                nc.vector.tensor_tensor(res[:, slot, i, :], ps[:, 0:C], res[:, slot, i, :], ALU.add).then_inc(dve_freed, 1)

            def route(s):
                ps = drain(s, "route")
                nc.vector.scalar_tensor_tensor(score[:, :], ps[0:1, 0:E], 1.0 / T, br_sb[:, :], ALU.mult, ALU.add)\
                  .then_inc(dve_freed, 1)
                wait_apart(dve, dve_freed, s.at(lambda n: fill(dve_fills, "route")(n) + 1))
                nc.vector.max(best[:, :], score[:, :]).then_inc(score_chain, 1)
                wait_apart(dve, score_chain, s.at(lambda n: n // DPB))
                nc.vector.max_index(which[:, :], best[:, :], score[:, :]).then_inc(expert_ready, 1)

            def step(s):
                n = s.n
                if n == -1:
                    measure_first(Step(-2))
                    apply_first(Step(-2))
                if has_ln2(n):
                    if n >= 2:
                        dve.wait_ge(act_filled, s.at(lambda n: fill(act_fills, "x2T")(n - 1) + 1))
                    apply_norm(s, 1, x1[:, (n - 1) % DPB, :, :], xn2, lambda n: n - 1, xn2_ready)
                if has_attn(n):
                    mask_weights(s, 0)
                if n + 2 < ND:
                    measure_first(s)
                if has_down(n):
                    finish(s, 0)
                if has_route(n):
                    route(s)
                if has_attn(n):
                    normalise(s, 0)
                if has_front(n):
                    ps = drain(s, "v")
                    nc.vector.tensor_tensor(
                        vaug[:, (n + 1) % 2, :, :, 0:D].rearrange("p i h d -> p i h d"),
                        ps[:, :].rearrange("p (i h d) -> p i h d", i=2, d=D),
                        bv[:, :].rearrange("p (a h d) -> p a h d", a=1, d=D).to_broadcast([P, 2, H, D]),
                        ALU.add).then_inc(dve_freed, 1)
                if has_down(n):
                    finish(s, 1)
                if has_attn(n):
                    split_attn(s, 0)
                    mask_weights(s, 1)
                    residual(s, 0)
                if n + 2 < ND:
                    apply_first(s)
                if has_attn(n):
                    normalise(s, 1)
                    split_attn(s, 1)
                    residual(s, 1)

            run(dve, step)

        @block.tensor
        def _(pe):
            pe.wait_ge(consts_ready, 2)
            for f in range(4):
                if f == 0:
                    pe.wait_ge(s_wqkv, 16)
                if f == 3:
                    pe.wait_ge(s_wout, 16)
                if f >= 2:
                    pe.wait_ge(setup_freed, f - 1)
                raw = wqkv_raw[:, 2 * f:2 * f + 2, :] if f < 3 else wout_raw
                for j in range(CJ):
                    for o in range(CJ):
                        last = nc.tensor.transpose(dve_bank[f % 2][:, (2 * j + o) * P:(2 * j + o + 1) * P],
                                                   raw[:, o, j * P:(j + 1) * P], ident[:, :])
                last.then_inc(setup_filled, 1)
            pe.wait_ge(silu_ready, 1)
            pe.wait_ge(s_wmod, 32)

            def wmod_cols(j, first, width):
                if first < 1024:
                    return wmod_a[:, j, first:first + width]
                return wmod_b[:, j, first - 1024:first - 1024 + width]

            for q, part in enumerate((0, 1, 3, 4)):
                for oj in range(CJ):
                    at = (q * CJ + oj) * B
                    for j in range(CJ):
                        last = nc.tensor.matmul(ctx_bank[:, at:at + B], wmod_cols(j, part * C + oj * P, P), scT[:, j, :],
                                                start=j == 0, stop=j == CJ - 1)
            last.then_inc(mod_filled, 1)
            for g, part in enumerate((2, 5)):
                for j in range(CJ):
                    last = nc.tensor.matmul(kv_bank[0:B, g * C:(g + 1) * C], scT[:, j, :], wmod_cols(j, part * C, C),
                                            start=j == 0, stop=j == CJ - 1)
            last.then_inc(mod_filled, 1)

            def product(dst, w, y, start, stop):
                (w_hi, w_lo), (y_hi, y_lo) = w, y
                nc.tensor.matmul(dst, w_hi, y_hi, start=start, stop=False)
                nc.tensor.matmul(dst, w_hi, y_lo, start=False, stop=False)
                return nc.tensor.matmul(dst, w_lo, y_hi, start=False, stop=stop)

            def act_fill(s, name):
                at = fill(act_fills, name)
                if at(s.n) >= 2:
                    pe.wait_ge(act_freed, s.at(lambda n: at(n) - 1))
                return act_bank[at(s.n) % 2]

            def dve_fill(s, name):
                at = fill(dve_fills, name)
                if at(s.n) >= 2:
                    pe.wait_ge(dve_freed, s.at(lambda n: at(n) - 1))
                return dve_bank[at(s.n) % 2]

            def transpose_norm(s, name, src):
                ps = act_fill(s, name)
                for j in range(CJ):
                    for i in range(2):
                        last = nc.tensor.transpose(ps[:, j * DUO + i * P:j * DUO + (i + 1) * P],
                                                   src[:, i, j * P:(j + 1) * P], ident[:, :])
                last.then_inc(act_filled, 1)

            def project_qk(s):
                pe.wait_ge(hT_split, s.at(lambda n: n + 2))
                for w in range(2):
                    ps = act_fill(s, f"qk{w}")
                    for g in range(CJ):
                        cols = slice((2 * w + g) * P, (2 * w + g + 1) * P)
                        for j in range(CJ):
                            last = product(ps[:, g * DUO:(g + 1) * DUO],
                                           (wqkvT_hi[:, j, cols], wqkvT_lo[:, j, cols]),
                                           (hT_hi[:, j, :], hT_lo[:, j, :]), j == 0, j == CJ - 1)
                    last.then_inc(act_filled, 1)

            def project_v(s):
                ps = dve_fill(s, "v")
                for i in range(2):
                    toks = slice(i * P, (i + 1) * P)
                    for j in range(CJ):
                        last = product(ps[:, i * C:(i + 1) * C], (hT_hi[:, j, toks], hT_lo[:, j, toks]),
                                       (wqkvT_hi[:, j, 2 * C:3 * C], wqkvT_lo[:, j, 2 * C:3 * C]), j == 0, j == CJ - 1)
                last.then_inc(dve_filled, 1)

            def features(s, w):
                pe.wait_ge(qk_split, s.at(lambda n: 2 * (n + 1) + w + 1))
                for j in range(4):
                    ps = act_fill(s, f"feat{w}{j}")
                    rows = slice(32 * j, 32 * j + 32)
                    for g in range(CJ):
                        last = product(ps[:, g * DUO:(g + 1) * DUO], (pbd_hi[rows, g, :], pbd_lo[rows, g, :]),
                                       (qkT_hi[rows, w, g, :], qkT_lo[rows, w, g, :]), True, True)
                    last.then_inc(act_filled, 1)

            def weights(s, i):
                fq, fk = feat[s.n % 2]
                toks = slice(i * P, (i + 1) * P)
                if i == 0:
                    pe.wait_ge(act_freed, s.at(lambda n: fill(act_fills, "feat13")(n - 1) + 1))
                for r in range(2):
                    for a in range(2):
                        rows = slice(a * M, (a + 1) * M)
                        if s.n > 0 or i > 0 or r > 0:
                            pe.wait_ge(aw_ready, s.at(lambda n: 4 * (2 * n + i) + 2 * r + a - 1))
                        for j in range(4):
                            last = nc.tensor.matmul(aw_bank[a][:, j * P:(j + 1) * P], fk[rows, 4 * r + j, toks],
                                                    fq[rows, 4 * r + j, toks], start=True, stop=True)
                        last.then_inc(aw_filled, 1)
                    if not is_last(s.n, i):
                        ps = act_fill(s, f"kp{i}{r}")
                        for j in range(4):
                            last = nc.tensor.transpose(ps[:, j * P:(j + 1) * P], fk[:, 4 * r + j, toks], ident[:, :])
                        last.then_inc(act_filled, 1)

            def context(s, i):
                fq = feat[s.n % 2][0]
                toks = slice(i * P, (i + 1) * P)
                first_chunk = s.n % DPB == 0 and i == 0
                va = vaug[:, s.n % 2, i, :, :]
                if s.n == 0 and i == 0:
                    pe.wait_ge(dve_freed, fill(dve_fills, "v")(-1) + 1)
                if s.n > 0 or i > 0:
                    pe.wait_ge(attn_ready, s.at(lambda n: 2 * n + i))
                if not first_chunk:
                    pe.wait_ge(kv_ready, s.at(lambda n: chunks_with_state(n, i - 1)))
                pe.wait_ge(aw_ready, s.at(lambda n: 4 * (2 * n + i) + 4))
                for pair in range(NPAIR):
                    if not first_chunk:
                        nc.tensor.matmul(ctx_bank[:, pair * 2 * VW:(pair + 1) * 2 * VW], fq[:, pair, toks], kvbd[:, pair, :],
                                         start=pair == 0, stop=False, skip_group_check=True)
                    for a in range(2):
                        h = 2 * pair + a
                        last = nc.tensor.matmul(ctx_bank[:, h * VW:(h + 1) * VW], awT[:, pair // 4, a, pair % 4, :],
                                                va[:, h, :], start=first_chunk and h == 0, stop=h == H - 1,
                                                skip_group_check=True)
                last.then_inc(ctx_filled, 1)

            def state(s, i):
                if is_last(s.n, i):
                    return
                first_chunk = s.n % DPB == 0 and i == 0
                if s.n > 0 or i > 0:
                    pe.wait_ge(kv_ready, s.at(lambda n: chunks_with_state(n, i) - 1))
                pe.wait_ge(act_freed, s.at(lambda n: fill(act_fills, f"kp{i}1")(n) + 1))
                va = vaug[:, s.n % 2, i, :, :].rearrange("p h w -> p (h w)")
                for pair in range(NPAIR):
                    cols = slice(pair * 2 * VW, (pair + 1) * 2 * VW)
                    last = nc.tensor.matmul(kv_bank[:, cols], kp[:, pair, :], va[:, cols],
                                            start=first_chunk and pair == 0, stop=pair == NPAIR - 1,
                                            skip_group_check=True)
                last.then_inc(kv_filled, 1)

            def transpose_attn(s, i):
                ps = dve_fill(s, f"aT{i}")
                pe.wait_ge(attn_ready, s.at(lambda n: 2 * n + i + 1))
                for j in range(CJ):
                    last = nc.tensor.transpose(ps[:, j * P:(j + 1) * P], attn[:, j * P:(j + 1) * P], ident[:, :])
                last.then_inc(dve_filled, 1)

            def project_out(s, i):
                if s.n % DPB == 0 and i == 0:
                    pe.wait_ge(wo_split, s.at(lambda n: n // DPB + 1))
                ps = dve_fill(s, f"o{i}")
                pe.wait_ge(dve_freed, s.at(lambda n: fill(dve_fills, f"aT{i}")(n) + 1))
                for j in range(CJ):
                    last = product(ps[:, 0:C], (aT_hi[:, j, :], aT_lo[:, j, :]), (wog_hi[:, j, :], wog_lo[:, j, :]),
                                   j == 0, j == CJ - 1)
                last.then_inc(dve_filled, 1)

            def route(s):
                ps = dve_fill(s, "route")
                pe.wait_ge(act_freed, s.at(lambda n: fill(act_fills, "x2T")(n) + 1))
                parts = [(j, d) for j in range(CJ) for d in range(DPB)]
                for at, (j, d) in enumerate(parts):
                    last = nc.tensor.matmul(ps[0:1, 0:E], hsum[:, j, d:d + 1], wr_sb[:, j, :],
                                            start=at == 0, stop=at == len(parts) - 1)
                last.then_inc(dve_filled, 1)

            def up(s, q):
                if q == 0:
                    pe.wait_ge(hF_split, s.at(lambda n: n - FFN_LAG + 1))
                    if s.n % DPB == 0:
                        pe.wait_ge(w1_split, s.at(lambda n: n // DPB))
                ps = act_fill(s, f"up{q}")
                slot = (s.n - FFN_LAG) % DPB
                for a in range(2):
                    for j in range(CJ):
                        last = product(ps[:, a * DUO:(a + 1) * DUO], (w1_hi[:, j, 2 * q + a, :], w1_lo[:, j, 2 * q + a, :]),
                                       (hF_hi[:, slot, j, :], hF_lo[:, slot, j, :]), j == 0, j == CJ - 1)
                last.then_inc(act_filled, 1)

            def down(s, i):
                if i == 0:
                    pe.wait_ge(h1_split, s.at(lambda n: 4 * (n - FFN_LAG)))
                    if s.n % DPB == 1:
                        pe.wait_ge(w2_split, s.at(lambda n: n // DPB))
                ps = dve_fill(s, f"down{i}")
                toks = slice(i * P, (i + 1) * P)
                for f in range(FC):
                    last = product(ps[:, 0:C], (h1_hi[:, f, toks], h1_lo[:, f, toks]), (w2_hi[:, f, :], w2_lo[:, f, :]),
                                   f == 0, f == FC - 1)
                last.then_inc(dve_filled, 1)

            def step(s):
                n = s.n
                if has_front(n):
                    pe.wait_ge(xn_ready, s.at(lambda n: 2 * (n + 2)))
                    transpose_norm(s, "xT", xn)
                if has_attn(n):
                    weights(s, 0)
                if has_ln2(n):
                    pe.wait_ge(xn2_ready, s.at(lambda n: 2 * n))
                    transpose_norm(s, "x2T", xn2)
                if has_down(n):
                    down(s, 0)
                if has_route(n):
                    route(s)
                if has_front(n):
                    project_qk(s)
                if has_attn(n):
                    context(s, 0)
                    state(s, 0)
                if has_front(n):
                    project_v(s)
                if has_down(n):
                    down(s, 1)
                if has_front(n):
                    features(s, 0)
                if has_attn(n):
                    transpose_attn(s, 0)
                    weights(s, 1)
                    project_out(s, 0)
                if has_front(n):
                    features(s, 1)
                if has_attn(n):
                    context(s, 1)
                    state(s, 1)
                if has_up(n):
                    up(s, 0)
                    up(s, 1)
                if has_attn(n):
                    transpose_attn(s, 1)
                if has_up(n):
                    up(s, 2)
                    up(s, 3)
                if has_attn(n):
                    project_out(s, 1)

            pe.wait_ge(pbd_ready, 5)
            run(pe, step)


_INS = ["L0_attn_x", "L0_attn_Wqkv", "L0_attn_bqkv", "L0_attn_Wout", "L0_attn_bout", "L0_attn_proj", "L0_ffn_Wr",
        "L0_ffn_br", "L0_ffn_W1", "L0_ffn_b1", "L0_ffn_W2", "L0_ffn_b2", "L0_c", "L0_wmod"]


def kernel(**inputs):
    import numpy as _np
    import concourse.bacc as _bacc
    from concourse.bass_utils import run_bass_kernel_spmd as _run

    nc = _bacc.Bacc("TRN2", target_bir_lowering=False, num_devices=1)
    arrays, args = {}, []
    for name in _INS:
        a = _np.ascontiguousarray(inputs[name])
        arrays[f"in_{name}"] = a
        args.append(nc.dram_tensor(f"in_{name}", a.shape, mybir.dt.from_np(a.dtype), kind="ExternalInput").ap())
    args.append(nc.dram_tensor("out_0", (B, T, C), F32, kind="ExternalOutput").ap())
    program(nc, *args)
    return _run(nc, [arrays], core_ids=[0]).results[0]["out_0"]
```

```python
from contextlib import ExitStack

import concourse.bass as bass
from concourse import mybir

F32 = mybir.dt.float32
F32R = mybir.dt.float32r
BF16 = mybir.dt.bfloat16
U32 = mybir.dt.uint32
ALU = mybir.AluOpType
ACT = mybir.ActivationFunctionType

P = 128
B, T, C = 8, 1024, 256
H, D, M = 16, 16, 64
E, F = 8, 1024
NPAIR = H // 2
CJ = C // P
FC = F // P
DUO = 2 * P
DPB = T // DUO
ND = B * DPB
VW = D + 1
PARTS = 3
EPS = 1e-5
DELTA = 1e-6
FFN_LAG = 5
LOOP = range(9, 13)
TURNS = 5


PRODUCTS = [(0, 0), (0, 1), (1, 0), (1, 1), (0, 2), (2, 0)]


class Step:

    def __init__(self, n, k=None):
        self.n, self.k = n, k

    def at(self, f):
        a = f(self.n)
        if self.k is None:
            return a
        slope = f(self.n + DPB) - a
        if slope == 0:
            return a
        assert f(self.n + 2 * DPB) - a == 2 * slope
        return self.k * slope + a


def has_front(n):
    return n + 1 < ND


def has_attn(n):
    return 0 <= n < ND


def has_ln2(n):
    return 1 <= n <= ND


def has_ffn(n):
    return FFN_LAG <= n < ND + FFN_LAG


def has_move(n):
    return DPB <= n < ND + DPB


def has_route(n):
    return n % DPB == 0 and DPB <= n <= ND


def is_last(n, i):
    return n % DPB == DPB - 1 and i == 1


def act_fills(n):
    out = []
    if has_front(n):
        out += ["xT"]
    if has_ffn(n):
        out += ["up0", "up1"]
    if has_attn(n):
        out += ["kp00", "kp01"]
    if has_front(n):
        out += ["qk0", "qk1"]
    if has_ffn(n):
        out += ["up2", "up3"]
    if has_ln2(n):
        out += ["x2T"]
    if has_attn(n) and not is_last(n, 1):
        out += ["kp10", "kp11"]
    if has_front(n):
        out += [f"feat1{j}" for j in range(4)] + [f"feat0{j}" for j in range(4)]
    return out


def dve_fills(n):
    out = []
    if has_attn(n):
        out += ["aw00", "aw01", "aw02", "aw03"]
    if has_front(n):
        out += ["v"]
    if has_attn(n):
        out += ["aw10", "aw11", "aT0", "aw12", "aw13", "o0"]
    if has_ffn(n):
        out += ["down0"]
    if has_attn(n):
        out += ["aT1"]
    if has_ffn(n):
        out += ["down1"]
    if has_attn(n):
        out += ["o1"]
    return out


def fill(fills, name):
    return lambda n: sum(len(fills(m)) for m in range(-1, n)) + fills(n).index(name)


def chunks_with_state(n, i):
    return (n // DPB) * (2 * DPB - 1) + 2 * (n % DPB) + i + 1


def program(nc, x, wqkv, bqkv, wout, bout, proj, wr, br, w1, b1, w2, b2, c, wmod, out):
    with ExitStack() as ctx:
        ctx.enter_context(nc.allow_non_contiguous_dma(reason="small bias and condition loads"))

        def sb(name, shape, dt=F32):
            return ctx.enter_context(nc.sbuf_tensor(name, shape, dt))

        def pb(name):
            return ctx.enter_context(nc.psum_tensor(name, [P, 512], F32))

        def sem(name):
            return ctx.enter_context(nc.semaphore(name))

        ident = sb("ident", [P, P])
        mask = sb("mask", [P, P])
        wqkvT_hi = sb("wqkvT_hi", [P, CJ, 3 * C], F32R)
        wqkvT_lo = sb("wqkvT_lo", [P, CJ, 3 * C], F32R)
        woT_hi = sb("woT_hi", [P, CJ, C], F32R)
        woT_lo = sb("woT_lo", [P, CJ, C], F32R)
        pbd = sb("pbd", [P, CJ, P])
        pbd_hi = sb("pbd_hi", [P, CJ, P], F32R)
        pbd_lo = sb("pbd_lo", [P, CJ, P], F32R)
        bqk = sb("bqk", [P, 4])
        bv = sb("bv", [P, C])
        bo = sb("bo", [P, C])
        gbo = sb("gbo", [P, C])
        wr_sb = sb("wr_sb", [P, CJ, E])
        br_sb = sb("br_sb", [1, E])
        cT = sb("cT", [P, CJ, B])
        scT = sb("scT", [P, CJ, B])
        modT = sb("modT", [P, 4, CJ, B])
        ga = sb("ga", [P, C])
        gb = sb("gb", [P, C])

        xin = sb("xin", [P, DPB, 2, C])
        x1 = sb("x1", [P, DPB, 2, C])
        res = sb("res", [P, 2, 2, C])
        eps = sb("eps", [P, 1])
        stats = [sb(f"stats{q}", [P, 2, 6]) for q in range(2)]
        mv = [sb(f"mv{q}", [P, 2, 2]) for q in range(2)]
        std = [sb(f"std{q}", [P, 2]) for q in range(2)]
        rstd = [sb(f"rstd{q}", [P, 2]) for q in range(2)]
        xn = sb("xn", [P, 2, C])
        xn2 = sb("xn2", [P, 2, C])
        h_full = sb("h_full", [P, CJ, DUO])
        hT_hi = sb("hT_hi", [P, CJ, DUO], F32R)
        hT_lo = sb("hT_lo", [P, CJ, DUO], F32R)
        hF_hi = sb("hF_hi", [P, DPB, CJ, DUO], F32R)
        hF_lo = sb("hF_lo", [P, DPB, CJ, DUO], F32R)
        hsum = sb("hsum", [P, CJ, DPB])
        qkT = sb("qkT", [P, 2, CJ, DUO])
        qkT_hi = sb("qkT_hi", [P, 2, CJ, DUO], F32R)
        qkT_lo = sb("qkT_lo", [P, 2, CJ, DUO], F32R)
        feat = [sb(f"feat_{w}", [P, NPAIR, DUO]) for w in "qk"]
        kp_full = sb("kp_full", [P, 2, 4, P])
        kp = [sb(f"kp{q}", [P, 2, 4, P], BF16) for q in range(PARTS)]
        v_full = sb("v_full", [P, 2, H, D])
        vaug = sb("vaug", [P, 2, 2, H, PARTS, VW], BF16)
        aw_full = sb("aw_full", [P, 2, 4, P])
        aw = [sb(f"aw{q}", [P, 2, 2, 4, P], BF16) for q in range(PARTS)]
        csum = sb("csum", [P, H, VW])
        kvbd = sb("kvbd", [P, NPAIR, 2 * VW])
        den = sb("den", [P, H])
        rden = sb("rden", [P, H])
        attn = sb("attn", [P, C])
        aT_hi = sb("aT_hi", [P, CJ, P], F32R)
        aT_lo = sb("aT_lo", [P, CJ, P], F32R)

        w1raw = sb("w1raw", [P, CJ, F])
        w1_hi = sb("w1_hi", [P, CJ, FC, P], F32R)
        w1_lo = sb("w1_lo", [P, CJ, FC, P], F32R)
        w2raw = w1raw[:, :, :].rearrange("p j f -> p (j f)").rearrange("p (f c) -> p f c", c=C)
        w2_hi = sb("w2_hi", [P, FC, C], F32R)
        w2_lo = sb("w2_lo", [P, FC, C], F32R)
        b1_sb = sb("b1_sb", [P, FC])
        b2_sb = sb("b2_sb", [P, C])
        gb2 = sb("gb2", [P, C])
        y_gated = sb("y_gated", [P, C])
        h1 = sb("h1", [P, 2, 2, DUO])
        h1_hi = sb("h1_hi", [P, FC, DUO], F32R)
        h1_lo = sb("h1_lo", [P, FC, DUO], F32R)
        score = sb("score", [1, E])
        best = sb("best", [1, E])
        which = sb("which", [1, E], U32)

        wqkv_raw = feat[0][:, :, :].rearrange("p a t -> p (a t)")[:, 0:6 * C].rearrange("p (o c) -> p o c", c=C)
        wout_raw = feat[1][:, :, :].rearrange("p a t -> p (a t)")[:, 0:2 * C].rearrange("p (o c) -> p o c", c=C)
        wmod_a = w1raw[:, :, :]
        wmod_b = h1[:, :, :, :].rearrange("p a b t -> p (a b t)").rearrange("p (j n) -> p j n", j=CJ)
        gate_raw, gate_abs = (aw_full[0:B, q, :, :].rearrange("p j t -> p (j t)").rearrange("p (g c) -> p g c", g=2)
                              for q in range(2))
        gate_row = xn2[0:B, :, :]

        gates_dram = nc.dram_tensor("gates_dram", (B, 2, C), F32, kind="Internal").ap()

        act_bank = [pb("act_bank0"), pb("act_bank1")]
        dve_bank = [pb("dve_bank0"), pb("dve_bank1"), pb("dve_bank2")]
        ctx_bank = [pb("ctx_low"), pb("ctx_high")]
        kv_bank = pb("kv_bank")

        s_wqkv, s_wout, s_wmod, s_small, s_pbd = sem("s_wqkv"), sem("s_wout"), sem("s_wmod"), sem("s_small"), sem("s_pbd")
        zeroed, consts_ready = sem("zeroed"), sem("consts_ready")
        silu_ready = sem("silu_ready")
        setup_filled, setup_freed = sem("setup_filled"), sem("setup_freed")
        mod_filled, mod_ready = sem("mod_filled"), sem("mod_ready")
        gate_chain, gates_stored = sem("gate_chain"), sem("gates_stored")
        pbd_ready = sem("pbd_ready")
        x_loaded = sem("x_loaded")
        ga_loaded, gb_loaded = sem("ga_loaded"), sem("gb_loaded")
        w1_loaded, w2_loaded, b1_loaded, b2_loaded = sem("w1_loaded"), sem("w2_loaded"), sem("b1_loaded"), sem("b2_loaded")
        out_stored = sem("out_stored")
        act_filled, act_freed = sem("act_filled"), sem("act_freed")
        dve_filled, dve_freed = sem("dve_filled"), sem("dve_freed")
        aw_chain, aw_split = sem("aw_chain"), sem("aw_split")
        kp_rest, kp_mid, kp_split = sem("kp_rest"), sem("kp_mid"), sem("kp_split")
        v_chain, v_split = sem("v_chain"), sem("v_split")
        route_filled, route_read = sem("route_filled"), sem("route_read")
        ctx_filled, attn_ready = sem("ctx_filled"), sem("attn_ready")
        kv_filled, kv_ready = sem("kv_filled"), sem("kv_ready")
        stats_chain = [sem("stats_chain0"), sem("stats_chain1")]
        std_ready = [sem("std_ready0"), sem("std_ready1")]
        rstd_ready = [sem("rstd_ready0"), sem("rstd_ready1")]
        xn_ready, xn2_ready = sem("xn_ready"), sem("xn2_ready")
        hT_split, hF_split, qk_split = sem("hT_split"), sem("hF_split"), sem("qk_split")
        norm_chain, aT_hi_ready = sem("norm_chain"), sem("aT_hi_ready")
        gbo_ready, gb2_ready = sem("gbo_ready"), sem("gb2_ready")
        x1_ready, result_ready = sem("x1_ready"), sem("result_ready")
        xb_ready, res_copied, x2_ready = sem("xb_ready"), sem("res_copied"), sem("x2_ready")
        score_chain, expert_ready = sem("score_chain"), sem("expert_ready")
        w1_hi_ready, w1_split = sem("w1_hi_ready"), sem("w1_split")
        w2_hi_ready, w2_split = sem("w2_hi_ready"), sem("w2_split")
        h1_split = sem("h1_split")

        x_v = x.rearrange("b (d i p) c -> p (b d) i c", i=2, p=P)
        out_v = out.rearrange("b (d i p) c -> p (b d) i c", i=2, p=P)
        gates_v = gates_dram.rearrange("b g c -> g b c")

        block = ctx.enter_context(nc.Block())

        def run(eng, step):
            for n in range(-1, LOOP[0]):
                step(Step(n))
            with eng.Fori(0, TURNS) as k:
                for n in LOOP:
                    step(Step(n, k))
            for n in range(LOOP[0] + DPB * TURNS, ND + FFN_LAG):
                step(Step(n))

        def wait_apart(eng, of, count):
            count = eng.to_reg(count) if not isinstance(count, int) else count
            eng.wait_ge(consts_ready, 1)
            eng.wait_ge(of, count)

        @block.sync
        def _(sp):
            sp.dma_start(wqkv_raw, wqkv.rearrange("(o p) c -> p o c", p=P)).then_inc(s_wqkv, 16)
            sp.dma_start(xin[:, 0, :, :], x_v[:, 0, :, :]).then_inc(x_loaded, 16)
            sp.dma_start(wout_raw, wout.rearrange("(o p) c -> p o c", p=P)).then_inc(s_wout, 16)
            for m in (1, 2):
                sp.wait_ge(x_loaded, 16 * m)
                sp.dma_start(xin[:, m, :, :], x_v[:, m, :, :]).then_inc(x_loaded, 16)
            sp.wait_ge(gate_chain, 3)
            sp.dma_start(gates_dram, gate_row[:, :, :]).then_inc(gates_stored, 16)
            sp.wait_ge(gates_stored, 16)
            sp.dma_start(ga[:, :], gates_v[0, 0:1, :].to_broadcast([P, C])).then_inc(ga_loaded, 16)

            def step(s):
                n = s.n
                if 0 <= n and n + 3 < ND:
                    if n >= 1:
                        wait_apart(sp, xn2_ready, s.at(lambda n: 2 * n))
                    wait_apart(sp, x_loaded, s.at(lambda n: 16 * (n + 3)))
                    sp.dma_start(xin[:, (n + 3) % DPB, :, :],
                                 x_v[:, bass.ds(s.at(lambda n: n + 3), 1), :, :].rearrange("p m i c -> p (m i) c"))\
                      .then_inc(x_loaded, 16)
                if has_route(n):
                    wait_apart(sp, expert_ready, s.at(lambda n: n // DPB))
                    expert = sp.value_load(which[0:1, 0:1], min_val=0, max_val=E - 1)
                    if n > DPB:
                        wait_apart(sp, w2_split, s.at(lambda n: n // DPB - 1))
                        wait_apart(sp, h1_split, s.at(lambda n: 4 * (n - FFN_LAG + 1)))
                    sp.dma_start(w1raw[:, :, :], w1[bass.ds(expert, 1), :, :].rearrange("e (j p) f -> p (e j) f", p=P))\
                      .then_inc(w1_loaded, 16)
                    sp.dma_start(b1_sb[:, :], b1[bass.ds(expert, 1), :].rearrange("e (p f) -> p (e f)", p=P))\
                      .then_inc(b1_loaded, 16)
                    wait_apart(sp, w1_split, s.at(lambda n: n // DPB))
                    sp.dma_start(w2raw[:, :, :], w2[bass.ds(expert, 1), :, :].rearrange("e (p f) c -> p (e f) c", p=P))\
                      .then_inc(w2_loaded, 16)
                    sp.dma_start(b2_sb[:, :], b2[bass.ds(expert, 1), :].to_broadcast([P, C])).then_inc(b2_loaded, 16)
                if has_ffn(n):
                    if n > FFN_LAG:
                        wait_apart(sp, out_stored, s.at(lambda n: 16 * (n - FFN_LAG)))
                    wait_apart(sp, result_ready, s.at(lambda n: 2 * (n - FFN_LAG + 1)))
                    sp.dma_start(out_v[:, bass.ds(s.at(lambda n: n - FFN_LAG), 1), :, :]
                                 .rearrange("p m i c -> p (m i) c"), res[:, (n - FFN_LAG) % 2, :, :])\
                      .then_inc(out_stored, 16)
                if has_route(n):
                    sp.dma_start(gb[:, :], gates_v[1, bass.ds(s.at(lambda n: n // DPB - 1), 1), :].to_broadcast([P, C]))\
                      .then_inc(gb_loaded, 16)
                if n % DPB == DPB - 1 and 0 <= n < ND - 1:
                    wait_apart(sp, x1_ready, s.at(lambda n: 2 * n + 2))
                    sp.dma_start(ga[:, :], gates_v[0, bass.ds(s.at(lambda n: n // DPB + 1), 1), :].to_broadcast([P, C]))\
                      .then_inc(ga_loaded, 16)

            run(sp, step)
            sp.wait_ge(out_stored, 16 * ND)

        @block.scalar
        def _(act):
            for j in range(CJ):
                act.dma_start(cT[:, j, :], c[:, j * P:(j + 1) * P].rearrange("b p -> p b")).then_inc(s_small, 16)
            act.dma_start(wmod_a, wmod.rearrange("(j p) n -> p j n", p=P)[:, :, 0:1024]).then_inc(s_wmod, 16)
            act.dma_start(wmod_b, wmod.rearrange("(j p) n -> p j n", p=P)[:, :, 1024:1536]).then_inc(s_wmod, 16)
            act.dma_start(wr_sb[:, :, :], wr.rearrange("(j p) e -> p j e", p=P)).then_inc(s_small, 16)
            act.dma_start(br_sb[:, :], br.rearrange("(a e) -> a e", a=1)).then_inc(s_small, 16)
            act.dma_start(bqk[:, :], bqkv[0:2 * C].rearrange("(o p) -> p o", p=P)).then_inc(s_small, 16)
            act.dma_start(bv[:, :], bqkv[2 * C:3 * C].rearrange("(a c) -> a c", a=1).to_broadcast([P, C])).then_inc(s_small, 16)
            act.dma_start(bo[:, :], bout.rearrange("(a c) -> a c", a=1).to_broadcast([P, C])).then_inc(s_small, 16)
            act.wait_ge(zeroed, 1)
            for h in range(H):
                act.dma_start(pbd[(h % 8) * D:(h % 8 + 1) * D, h // 8, (h % 2) * M:(h % 2 + 1) * M], proj[h, :, :])\
                   .then_inc(s_pbd, 16)
            act.wait_ge(s_small, 16 * 7)
            nc.scalar.activation(scT[:, :, :], cT[:, :, :], ACT.Silu).then_inc(silu_ready, 1)

            def drain(s, name):
                if name in ("xT", "x2T"):
                    wait_apart(act, act_filled, s.at(lambda n: fill(act_fills, name)(n) + 1))
                else:
                    act.wait_ge(act_filled, s.at(lambda n: fill(act_fills, name)(n) + 1))
                return act_bank[fill(act_fills, name)(s.n) % 2]

            def kp_copy(s, i):
                for half in range(2):
                    ps = drain(s, f"kp{i}{half}")
                    if half == 0 and (s.n > 0 or i > 0):
                        act.wait_ge(kp_split, s.at(lambda n: chunks_with_state(n, i) - 1))
                        act.wait_ge(kv_filled, s.at(lambda n: chunks_with_state(n, i) - 1))
                    src = ps[:, :].rearrange("p (a s) -> p a s", s=P)
                    nc.scalar.activation(kp_full[:, half, :, :], src, ACT.Copy)
                    nc.scalar.activation(kp[0][:, half, :, :], src, ACT.Copy).then_inc(act_freed, 1)

            def kp_middle(s, i):
                for half in range(2):
                    act.wait_ge(kp_rest, s.at(lambda n: 2 * chunks_with_state(n, i) + half - 1))
                    nc.scalar.activation(kp[1][:, half, :, :], kp_full[:, half, :, :], ACT.Copy).then_inc(kp_mid, 1)

            def modulate(s, ps, full, hi, shift, gain, batch, sums):
                for j in range(CJ):
                    src = ps[:, j * DUO:(j + 1) * DUO]
                    scale = modT[:, gain, j, bass.ds(batch, 1)]
                    bias = modT[:, shift, j, bass.ds(batch, 1)]
                    nc.scalar.activation(full[:, j, :], src, ACT.Identity, bias=bias, scale=scale,
                                         accum_out=None if sums is None else sums[:, j:j + 1])
                    last = nc.scalar.activation(hi[:, j, :], src, ACT.Identity, bias=bias, scale=scale)
                return last

            def state_copy(s, i):
                act.wait_ge(kv_filled, s.at(lambda n: chunks_with_state(n, i)))
                ps = kv_bank[:, 0:NPAIR * 2 * VW].rearrange("p (a w) -> p a w", w=2 * VW)
                nc.scalar.activation(kvbd[0:M, :, 0:VW], ps[0:M, :, 0:VW], ACT.Copy)
                nc.scalar.activation(kvbd[M:P, :, VW:2 * VW], ps[M:P, :, VW:2 * VW], ACT.Copy).then_inc(kv_ready, 1)

            def features(s, w):
                dst = feat[w][:, :, :].rearrange("p (g j) t -> p g j t", j=4)
                for j in range(4):
                    ps = drain(s, f"feat{w}{j}")
                    nc.scalar.activation(dst[:, :, j, :], ps[:, :].rearrange("p (g t) -> p g t", t=DUO), ACT.Relu)\
                      .then_inc(act_freed, 1)

            def deviation(s, q, duo):
                act.wait_ge(stats_chain[q], s.at(lambda n: 4 * duo(n) + 4))
                nc.scalar.activation(std[q][:, :], mv[q][:, :, 1], ACT.Sqrt, bias=eps[:, :]).then_inc(std_ready[q], 1)

            def up(s, q):
                if s.n % DPB == 1 and q == 0:
                    act.wait_ge(b1_loaded, s.at(lambda n: 16 * (n // DPB)))
                ps = drain(s, f"up{q}")
                if s.n > FFN_LAG or q >= 2:
                    act.wait_ge(h1_split, s.at(lambda n: 4 * (n - FFN_LAG) + q - 1))
                for a in range(2):
                    src = ps[:, a * DUO:(a + 1) * DUO]
                    bias = b1_sb[:, 2 * q + a:2 * q + a + 1]
                    nc.scalar.activation(h1[:, q % 2, a, :], src, ACT.Relu, bias=bias)
                    last = nc.scalar.activation(h1_hi[:, 2 * q + a, :], src, ACT.Relu, bias=bias)
                last.then_inc(act_freed, 1)

            def step(s):
                n = s.n
                if n == -1:
                    act.wait_ge(zeroed, 7)
                    deviation(Step(-2), 0, lambda n: n + 2)
                if has_front(n):
                    ps = drain(s, "xT")
                    if n >= 2:
                        wait_apart(act, hF_split, s.at(lambda n: n - 1))
                    elif n >= 0:
                        wait_apart(act, hT_split, n + 1)
                    modulate(s, ps, h_full, hT_hi, 0, 1, s.at(lambda n: (n + 1) // DPB), None).then_inc(act_freed, 1)
                if has_ln2(n):
                    deviation(s, 1, lambda n: n - 1)
                if has_ffn(n):
                    up(s, 0)
                    up(s, 1)
                if has_attn(n):
                    kp_copy(s, 0)
                if has_front(n):
                    for w in range(2):
                        ps = drain(s, f"qk{w}")
                        if n >= 0:
                            act.wait_ge(qk_split, s.at(lambda n: 2 * (n + 1)))
                        for g in range(CJ):
                            src = ps[:, g * DUO:(g + 1) * DUO]
                            bias = bqk[:, 2 * w + g:2 * w + g + 1]
                            nc.scalar.activation(qkT[:, w, g, :], src, ACT.Identity, bias=bias)
                            last = nc.scalar.activation(qkT_hi[:, w, g, :], src, ACT.Identity, bias=bias)
                        last.then_inc(act_freed, 1)
                if has_move(n):
                    act.wait_ge(xn2_ready, s.at(lambda n: 2 * (n - DPB + 1)))
                    if n > FFN_LAG:
                        act.wait_ge(out_stored, s.at(lambda n: 16 * (n - FFN_LAG)))
                    nc.scalar.activation(res[:, (n - DPB) % 2, :, :], x1[:, (n - DPB) % DPB, :, :], ACT.Copy)\
                      .then_inc(res_copied, 1)
                if has_attn(n):
                    kp_middle(s, 0)
                if has_ffn(n) and n % DPB == 1:
                    act.wait_ge(w2_loaded, s.at(lambda n: 16 * (n // DPB)))
                    if n > FFN_LAG:
                        act.wait_ge(dve_freed, s.at(lambda n: fill(dve_fills, "down1")(n - 1) + 1))
                    nc.scalar.activation(w2_hi[:, :, :], w2raw[:, :, :], ACT.Copy).then_inc(w2_hi_ready, 1)
                if n + 2 < ND:
                    deviation(s, 0, lambda n: n + 2)
                if has_ffn(n):
                    up(s, 2)
                if has_attn(n):
                    state_copy(s, 0)
                if has_ffn(n):
                    up(s, 3)
                if has_ln2(n):
                    ps = drain(s, "x2T")
                    if has_front(n):
                        wait_apart(act, hT_split, s.at(lambda n: n + 2))
                    else:
                        wait_apart(act, hF_split, n - 1)
                    slot = (n - 1) % DPB
                    modulate(s, ps, h_full, hF_hi[:, slot, :, :], 2, 3, s.at(lambda n: (n - 1) // DPB),
                             hsum[:, :, slot]).then_inc(act_freed, 1)
                if has_attn(n) and not is_last(n, 1):
                    kp_copy(s, 1)
                if has_front(n):
                    features(s, 1)
                if has_attn(n) and not is_last(n, 1):
                    kp_middle(s, 1)
                if has_route(n):
                    act.wait_ge(w1_loaded, s.at(lambda n: 16 * (n // DPB)))
                    for j in range(CJ):
                        nc.scalar.activation(w1_hi[:, j, :, :], w1raw[:, j, :].rearrange("p (q f) -> p f q", f=FC),
                                             ACT.Copy).then_inc(w1_hi_ready, 1)
                if has_front(n):
                    features(s, 0)
                if has_attn(n) and not is_last(n, 1):
                    state_copy(s, 1)

            run(act, step)

        @block.gpsimd
        def _(pool):
            nc.gpsimd.memset(pbd[:, :, :], 0.0).then_inc(zeroed, 1)
            nc.gpsimd.memset(ident[:, :], 0.0).then_inc(zeroed, 1)
            nc.gpsimd.memset(mask[:, :], 1.0).then_inc(zeroed, 1)
            nc.gpsimd.memset(vaug[:, :, :, :, 0, D:VW], 1.0).then_inc(zeroed, 1)
            nc.gpsimd.memset(vaug[:, :, :, :, 1:PARTS, D:VW], 0.0).then_inc(zeroed, 1)
            nc.gpsimd.memset(kvbd[:, :, :], 0.0).then_inc(zeroed, 1)
            nc.gpsimd.memset(eps[:, :], EPS).then_inc(zeroed, 1)
            pool.wait_ge(zeroed, 7)
            nc.gpsimd.affine_select(out=ident[:, :], in_=ident[:, :], compare_op=ALU.not_equal, fill=1.0, base=0,
                                    pattern=[[-1, P]], channel_multiplier=1).then_inc(consts_ready, 1)
            nc.gpsimd.affine_select(out=mask[:, :], in_=mask[:, :], compare_op=ALU.is_ge, fill=0.0, base=0,
                                    pattern=[[1, P]], channel_multiplier=-1).then_inc(consts_ready, 1)

            def minus_hi(lo, full, hi):
                return nc.gpsimd.tensor_tensor(lo, full, hi.bitcast(F32), ALU.subtract)

            def kp_remainder(s, i):
                for half in range(2):
                    pool.wait_ge(act_freed, s.at(lambda n: fill(act_fills, f"kp{i}{half}")(n) + 1))
                    nc.gpsimd.tensor_tensor(kp_full[:, half, :, :], kp_full[:, half, :, :], kp[0][:, half, :, :],
                                            ALU.subtract).then_inc(kp_rest, 1)

            def kp_third(s, i):
                for half in range(2):
                    pool.wait_ge(kp_mid, s.at(lambda n: 2 * chunks_with_state(n, i) + half - 1))
                    last = nc.gpsimd.tensor_tensor(kp[2][:, half, :, :], kp_full[:, half, :, :], kp[1][:, half, :, :],
                                                   ALU.subtract)
                last.then_inc(kp_split, 1)

            def h1_lower(s, q):
                pool.wait_ge(act_freed, s.at(lambda n: fill(act_fills, f"up{q}")(n) + 1))
                minus_hi(h1_lo[:, 2 * q:2 * q + 2, :], h1[:, q % 2, :, :], h1_hi[:, 2 * q:2 * q + 2, :]).then_inc(h1_split, 1)

            def step(s):
                n = s.n
                if has_front(n):
                    pool.wait_ge(act_freed, s.at(lambda n: fill(act_fills, "xT")(n) + 1))
                    minus_hi(hT_lo[:, :, :], h_full[:, :, :], hT_hi[:, :, :]).then_inc(hT_split, 1)
                if has_attn(n) and n % DPB == 0:
                    if n == 0:
                        pool.wait_ge(s_small, 16 * 7)
                    else:
                        pool.wait_ge(xb_ready, s.at(lambda n: 2 * n))
                    pool.wait_ge(ga_loaded, s.at(lambda n: 16 * (n // DPB + 1)))
                    nc.gpsimd.tensor_tensor(gbo[:, :], bo[:, :], ga[:, :], ALU.mult).then_inc(gbo_ready, 1)
                if has_ffn(n):
                    if n % DPB == 1:
                        if n > FFN_LAG:
                            pool.wait_ge(x2_ready, s.at(lambda n: 2 * (n - FFN_LAG)))
                        pool.wait_ge(b2_loaded, s.at(lambda n: 16 * (n // DPB)))
                        pool.wait_ge(gb_loaded, s.at(lambda n: 16 * (n // DPB)))
                        nc.gpsimd.tensor_tensor(gb2[:, :], b2_sb[:, :], gb[:, :], ALU.mult).then_inc(gb2_ready, 1)
                        pool.wait_ge(gb2_ready, s.at(lambda n: n // DPB))
                    slot = (n - FFN_LAG) % 2
                    pool.wait_ge(res_copied, s.at(lambda n: n - FFN_LAG + 1))
                    for i in range(2):
                        nc.gpsimd.tensor_tensor(res[:, slot, i, :], res[:, slot, i, :], gb2[:, :], ALU.add)\
                          .then_inc(x2_ready, 1)
                    h1_lower(s, 0)
                    h1_lower(s, 1)
                if has_attn(n):
                    kp_remainder(s, 0)
                    pool.wait_ge(xn_ready, s.at(lambda n: 2 * (n + 1)))
                    if n % DPB == 0:
                        pool.wait_ge(gbo_ready, s.at(lambda n: n // DPB + 1))
                    for i in range(2):
                        nc.gpsimd.tensor_tensor(xin[:, n % DPB, i, :], xin[:, n % DPB, i, :], gbo[:, :], ALU.add)\
                          .then_inc(xb_ready, 1)
                if has_front(n):
                    for w in range(2):
                        pool.wait_ge(act_freed, s.at(lambda n: fill(act_fills, f"qk{w}")(n) + 1))
                        minus_hi(qkT_lo[:, w, :, :], qkT[:, w, :, :], qkT_hi[:, w, :, :]).then_inc(qk_split, 1)
                if has_attn(n):
                    kp_third(s, 0)
                if has_ffn(n):
                    if n % DPB == 1:
                        pool.wait_ge(w2_hi_ready, s.at(lambda n: n // DPB))
                        minus_hi(w2_lo[:, :, :], w2raw[:, :, :], w2_hi[:, :, :]).then_inc(w2_split, 1)
                    h1_lower(s, 2)
                    h1_lower(s, 3)
                if has_ln2(n):
                    pool.wait_ge(act_freed, s.at(lambda n: fill(act_fills, "x2T")(n) + 1))
                    slot = (n - 1) % DPB
                    minus_hi(hF_lo[:, slot, :, :], h_full[:, :, :], hF_hi[:, slot, :, :]).then_inc(hF_split, 1)
                if has_attn(n) and not is_last(n, 1):
                    kp_remainder(s, 1)
                    kp_third(s, 1)
                if has_route(n):
                    for j in range(CJ):
                        pool.wait_ge(w1_hi_ready, s.at(lambda n: 2 * (n // DPB - 1) + j + 1))
                        last = minus_hi(w1_lo[:, j, :, :], w1raw[:, j, :].rearrange("p (q f) -> p f q", f=FC),
                                        w1_hi[:, j, :, :])
                    last.then_inc(w1_split, 1)

            run(pool, step)

        @block.vector
        def _(dve):
            for f in range(4):
                dve.wait_ge(setup_filled, f + 1)
                ps = dve_bank[f % 2]
                if f < 3:
                    dst = slice(f * C, (f + 1) * C)
                    hi, lo = wqkvT_hi[:, :, dst], wqkvT_lo[:, :, dst]
                else:
                    hi, lo = woT_hi[:, :, :], woT_lo[:, :, :]
                src = ps[:, :].rearrange("p (j o) -> p j o", j=CJ)
                nc.vector.tensor_copy(hi, src).then_inc(pbd_ready, 1)
                dve.wait_ge(pbd_ready, f + 1)
                nc.vector.tensor_tensor(lo, src, hi.bitcast(F32), ALU.subtract).then_inc(setup_freed, 1)
            dve.wait_ge(s_pbd, 16 * H)
            nc.vector.tensor_copy(pbd_hi[:, :, :], pbd[:, :, :]).then_inc(pbd_ready, 1)
            dve.wait_ge(pbd_ready, 5)
            nc.vector.tensor_tensor(pbd_lo[:, :, :], pbd[:, :, :], pbd_hi[:, :, :].bitcast(F32), ALU.subtract)\
              .then_inc(pbd_ready, 1)
            dve.wait_ge(mod_filled, 1)
            ps = ctx_bank[0][:, 0:4 * CJ * B].rearrange("p (q j b) -> p q j b", q=4, j=CJ)
            for q in range(4):
                nc.vector.tensor_scalar(modT[:, q, :, :], ps[:, q, :, :], float(q % 2), None, ALU.add).then_inc(mod_ready, 1)
            dve.wait_ge(mod_filled, 2)
            nc.vector.tensor_copy(gate_raw[:, :, :], kv_bank[0:B, :].rearrange("p (q c) -> p q c", q=2)).then_inc(gate_chain, 1)
            dve.wait_ge(gate_chain, 1)
            nc.vector.scalar_tensor_tensor(gate_abs, gate_raw, -1.0, gate_raw, ALU.mult, ALU.max).then_inc(mod_ready, 1)
            dve.wait_ge(mod_ready, 5)
            nc.vector.tensor_scalar(gate_abs, gate_abs, 0.25, None, ALU.max).then_inc(mod_ready, 1)
            nc.vector.tensor_scalar(gate_row[:, :, :], gate_raw[:, :, :], 0.0, 2.0, ALU.is_ge, ALU.mult).then_inc(gate_chain, 1)
            dve.wait_ge(mod_ready, 6)
            dve.wait_ge(gate_chain, 2)
            nc.vector.scalar_tensor_tensor(gate_row[:, :, :], gate_row[:, :, :], -1.0, gate_abs[:, :, :],
                                           ALU.add, ALU.mult).then_inc(gate_chain, 1)

            def drain(s, name):
                dve.wait_ge(dve_filled, s.at(lambda n: fill(dve_fills, name)(n) + 1))
                return dve_bank[fill(dve_fills, name)(s.n) % 3]

            def measure(s, q, i, src, duo):
                nc.vector.bn_stats(stats[q][:, i, :], src).then_inc(stats_chain[q], 1)
                wait_apart(dve, stats_chain[q], s.at(lambda n: 4 * duo(n) + 2 * i + 1))
                nc.vector.bn_aggr(mv[q][:, i, :], stats[q][:, i, :]).then_inc(stats_chain[q], 1)

            def apply_norm(s, q, src, dst, duo, done):
                dve.wait_ge(std_ready[q], s.at(lambda n: duo(n) + 1))
                nc.vector.reciprocal(rstd[q][:, :], std[q][:, :]).then_inc(rstd_ready[q], 1)
                dve.wait_ge(rstd_ready[q], s.at(lambda n: duo(n) + 1))
                for i in range(2):
                    nc.vector.tensor_scalar(dst[:, i, :], src[:, i, :], mv[q][:, i, 0:1], rstd[q][:, i:i + 1],
                                            ALU.subtract, ALU.mult).then_inc(done, 1)

            def measure_first(s):
                dve.wait_ge(x_loaded, s.at(lambda n: 16 * (n + 3)))
                for i in range(2):
                    measure(s, 0, i, xin[:, (s.n + 2) % DPB, i, :], lambda n: n + 2)

            def apply_first(s):
                if s.n >= -1:
                    dve.wait_ge(act_filled, s.at(lambda n: fill(act_fills, "xT")(n) + 1))
                apply_norm(s, 0, xin[:, (s.n + 2) % DPB, :, :], xn, lambda n: n + 2, xn_ready)

            def split_weights(s, i, r):
                done = lambda n: 2 * (2 * n + i) + r
                if s.n > 0 or i > 0 or r > 0:
                    dve.wait_ge(aw_split, s.at(done))
                for a in range(2):
                    ps = drain(s, f"aw{i}{2 * r + a}")
                    nc.vector.tensor_tensor(aw_full[:, a, :, :], ps[:, :].rearrange("p (j t) -> p j t", t=P),
                                            mask[:, :].rearrange("p (a t) -> p a t", a=1).to_broadcast([P, 4, P]),
                                            ALU.mult).then_inc(dve_freed, 1)
                dve.wait_ge(dve_freed, s.at(lambda n: fill(dve_fills, f"aw{i}{2 * r + 1}")(n) + 1))
                nc.vector.tensor_copy(aw[0][:, r, :, :, :], aw_full[:, :, :, :]).then_inc(aw_chain, 1)
                dve.wait_ge(aw_chain, s.at(lambda n: 3 * done(n) + 1))
                nc.vector.tensor_tensor(aw_full[:, :, :, :], aw_full[:, :, :, :], aw[0][:, r, :, :, :], ALU.subtract)\
                  .then_inc(aw_chain, 1)
                dve.wait_ge(aw_chain, s.at(lambda n: 3 * done(n) + 2))
                nc.vector.tensor_copy(aw[1][:, r, :, :, :], aw_full[:, :, :, :]).then_inc(aw_chain, 1)
                dve.wait_ge(aw_chain, s.at(lambda n: 3 * done(n) + 3))
                nc.vector.tensor_tensor(aw[2][:, r, :, :, :], aw_full[:, :, :, :], aw[1][:, r, :, :, :], ALU.subtract)\
                  .then_inc(aw_split, 1)

            def split_values(s):
                if s.n >= 0:
                    dve.wait_ge(v_split, s.at(lambda n: n + 1))
                ps = drain(s, "v")
                nc.vector.tensor_tensor(
                    v_full[:, :, :, :], ps[:, :].rearrange("p (i h d) -> p i h d", i=2, d=D),
                    bv[:, :].rearrange("p (a h d) -> p a h d", a=1, d=D).to_broadcast([P, 2, H, D]),
                    ALU.add).then_inc(dve_freed, 1)
                part = [vaug[:, (s.n + 1) % 2, :, :, q, 0:D] for q in range(PARTS)]
                dve.wait_ge(dve_freed, s.at(lambda n: fill(dve_fills, "v")(n) + 1))
                nc.vector.tensor_copy(part[0], v_full[:, :, :, :]).then_inc(v_chain, 1)
                dve.wait_ge(v_chain, s.at(lambda n: 3 * (n + 1) + 1))
                nc.vector.tensor_tensor(v_full[:, :, :, :], v_full[:, :, :, :], part[0], ALU.subtract).then_inc(v_chain, 1)
                dve.wait_ge(v_chain, s.at(lambda n: 3 * (n + 1) + 2))
                nc.vector.tensor_copy(part[1], v_full[:, :, :, :]).then_inc(v_chain, 1)
                dve.wait_ge(v_chain, s.at(lambda n: 3 * (n + 1) + 3))
                nc.vector.tensor_tensor(part[2], v_full[:, :, :, :], part[1], ALU.subtract).then_inc(v_split, 1)

            def normalise(s, i):
                if s.n > 0 or i > 0:
                    dve.wait_ge(attn_ready, s.at(lambda n: 2 * n + i))
                dve.wait_ge(ctx_filled, s.at(lambda n: 2 * n + i + 1))
                for b in range(2):
                    ps = ctx_bank[b][:, 0:H // 2 * PARTS * VW].rearrange("p (h q w) -> p h w q", q=PARTS, w=VW)
                    nc.vector.tensor_reduce(csum[:, b * H // 2:(b + 1) * H // 2, :], ps, mybir.AxisListType.X, ALU.add)\
                      .then_inc(norm_chain, 1)
                dve.wait_ge(norm_chain, s.at(lambda n: 4 * (2 * n + i) + 2))
                nc.vector.tensor_scalar(den[:, :], csum[:, :, D], DELTA, None, ALU.add).then_inc(norm_chain, 1)
                dve.wait_ge(norm_chain, s.at(lambda n: 4 * (2 * n + i) + 3))
                nc.vector.reciprocal(rden[:, :], den[:, :]).then_inc(norm_chain, 1)
                dve.wait_ge(norm_chain, s.at(lambda n: 4 * (2 * n + i) + 4))
                nc.vector.tensor_tensor(attn[:, :].rearrange("p (h d) -> p h d", d=D), csum[:, :, 0:D],
                                        rden[:, :].rearrange("p (h a) -> p h a", a=1).to_broadcast([P, H, D]),
                                        ALU.mult).then_inc(attn_ready, 1)

            def split_attn(s, i):
                ps = drain(s, f"aT{i}")
                src = ps[:, 0:C].rearrange("p (j t) -> p j t", t=P)
                nc.vector.tensor_copy(aT_hi[:, :, :], src).then_inc(aT_hi_ready, 1)
                dve.wait_ge(aT_hi_ready, s.at(lambda n: 2 * n + i + 1))
                nc.vector.tensor_tensor(aT_lo[:, :, :], src, aT_hi[:, :, :].bitcast(F32), ALU.subtract).then_inc(dve_freed, 1)

            def residual(s, i):
                ps = drain(s, f"o{i}")
                slot = s.n % DPB
                dve.wait_ge(xb_ready, s.at(lambda n: 2 * n + i + 1))
                if has_move(s.n) and i == 0:
                    dve.wait_ge(res_copied, s.at(lambda n: n - DPB + 1))
                if s.n % DPB == 0 and i == 0:
                    dve.wait_ge(ga_loaded, s.at(lambda n: 16 * (n // DPB + 1)))
                nc.vector.tensor_tensor(x1[:, slot, i, :], ps[:, 0:C], ga[:, :], ALU.mult).then_inc(dve_freed, 1)
                dve.wait_ge(dve_freed, s.at(lambda n: fill(dve_fills, f"o{i}")(n) + 1))
                nc.vector.tensor_tensor(x1[:, slot, i, :], x1[:, slot, i, :], xin[:, slot, i, :], ALU.add)\
                  .then_inc(x1_ready, 1)
                dve.wait_ge(x1_ready, s.at(lambda n: 2 * n + i + 1))
                measure(s, 1, i, x1[:, slot, i, :], lambda n: n)

            def finish(s, i):
                done = lambda n: 2 * (n - FFN_LAG) + i
                slot = (s.n - FFN_LAG) % 2
                if s.n % DPB == 1 and i == 0:
                    dve.wait_ge(gb_loaded, s.at(lambda n: 16 * (n // DPB)))
                if s.n > FFN_LAG or i > 0:
                    dve.wait_ge(result_ready, s.at(done))
                ps = drain(s, f"down{i}")
                nc.vector.tensor_tensor(y_gated[:, :], ps[:, 0:C], gb[:, :], ALU.mult).then_inc(dve_freed, 1)
                dve.wait_ge(x2_ready, s.at(lambda n: done(n) + 1))
                dve.wait_ge(dve_freed, s.at(lambda n: fill(dve_fills, f"down{i}")(n) + 1))
                nc.vector.tensor_tensor(res[:, slot, i, :], y_gated[:, :], res[:, slot, i, :], ALU.add)\
                  .then_inc(result_ready, 1)

            def route(s):
                dve.wait_ge(route_filled, s.at(lambda n: n // DPB))
                nc.vector.scalar_tensor_tensor(score[:, :], ctx_bank[0][0:1, 0:E], 1.0 / T, br_sb[:, :], ALU.mult, ALU.add)\
                  .then_inc(route_read, 1)
                wait_apart(dve, route_read, s.at(lambda n: n // DPB))
                nc.vector.max(best[:, :], score[:, :]).then_inc(score_chain, 1)
                wait_apart(dve, score_chain, s.at(lambda n: n // DPB))
                nc.vector.max_index(which[:, :], best[:, :], score[:, :]).then_inc(expert_ready, 1)

            def step(s):
                n = s.n
                if n == -1:
                    measure_first(Step(-2))
                    apply_first(Step(-2))
                if has_attn(n):
                    split_weights(s, 0, 0)
                    split_weights(s, 0, 1)
                if has_ln2(n):
                    if n >= 2:
                        dve.wait_ge(act_filled, s.at(lambda n: fill(act_fills, "x2T")(n - 1) + 1))
                    apply_norm(s, 1, x1[:, (n - 1) % DPB, :, :], xn2, lambda n: n - 1, xn2_ready)
                if n + 2 < ND:
                    measure_first(s)
                if has_attn(n):
                    normalise(s, 0)
                if has_front(n):
                    split_values(s)
                if has_attn(n):
                    split_weights(s, 1, 0)
                if has_route(n):
                    route(s)
                if has_attn(n):
                    split_attn(s, 0)
                    split_weights(s, 1, 1)
                    residual(s, 0)
                if n + 2 < ND:
                    apply_first(s)
                if has_ffn(n):
                    finish(s, 0)
                if has_attn(n):
                    normalise(s, 1)
                    split_attn(s, 1)
                if has_ffn(n):
                    finish(s, 1)
                if has_attn(n):
                    residual(s, 1)

            run(dve, step)

        @block.tensor
        def _(pe):
            pe.wait_ge(consts_ready, 2)
            for f in range(4):
                if f == 0:
                    pe.wait_ge(s_wqkv, 16)
                if f == 3:
                    pe.wait_ge(s_wout, 16)
                if f >= 2:
                    pe.wait_ge(setup_freed, f - 1)
                raw = wqkv_raw[:, 2 * f:2 * f + 2, :] if f < 3 else wout_raw
                for j in range(CJ):
                    for o in range(CJ):
                        last = nc.tensor.transpose(dve_bank[f % 2][:, (2 * j + o) * P:(2 * j + o + 1) * P],
                                                   raw[:, o, j * P:(j + 1) * P], ident[:, :])
                last.then_inc(setup_filled, 1)
            pe.wait_ge(silu_ready, 1)
            pe.wait_ge(s_wmod, 32)

            def wmod_cols(j, first, width):
                if first < 1024:
                    return wmod_a[:, j, first:first + width]
                return wmod_b[:, j, first - 1024:first - 1024 + width]

            for q, part in enumerate((0, 1, 3, 4)):
                for oj in range(CJ):
                    at = (q * CJ + oj) * B
                    for j in range(CJ):
                        last = nc.tensor.matmul(ctx_bank[0][:, at:at + B], wmod_cols(j, part * C + oj * P, P), scT[:, j, :],
                                                start=j == 0, stop=j == CJ - 1)
            last.then_inc(mod_filled, 1)
            for g, part in enumerate((2, 5)):
                for j in range(CJ):
                    last = nc.tensor.matmul(kv_bank[0:B, g * C:(g + 1) * C], scT[:, j, :], wmod_cols(j, part * C, C),
                                            start=j == 0, stop=j == CJ - 1)
            last.then_inc(mod_filled, 1)

            def product(dst, w, y, start, stop):
                (w_hi, w_lo), (y_hi, y_lo) = w, y
                nc.tensor.matmul(dst, w_hi, y_hi, start=start, stop=False)
                nc.tensor.matmul(dst, w_hi, y_lo, start=False, stop=False)
                return nc.tensor.matmul(dst, w_lo, y_hi, start=False, stop=stop)

            def act_fill(s, name):
                at = fill(act_fills, name)
                if at(s.n) >= 2:
                    pe.wait_ge(act_freed, s.at(lambda n: at(n) - 1))
                return act_bank[at(s.n) % 2]

            def dve_fill(s, name):
                at = fill(dve_fills, name)
                if at(s.n) >= 3:
                    pe.wait_ge(dve_freed, s.at(lambda n: at(n) - 2))
                return dve_bank[at(s.n) % 3]

            def transpose_norm(s, name, src):
                ps = act_fill(s, name)
                for j in range(CJ):
                    for i in range(2):
                        last = nc.tensor.transpose(ps[:, j * DUO + i * P:j * DUO + (i + 1) * P],
                                                   src[:, i, j * P:(j + 1) * P], ident[:, :])
                last.then_inc(act_filled, 1)

            def project_qk(s):
                pe.wait_ge(hT_split, s.at(lambda n: n + 2))
                for w in range(2):
                    ps = act_fill(s, f"qk{w}")
                    for g in range(CJ):
                        cols = slice((2 * w + g) * P, (2 * w + g + 1) * P)
                        for j in range(CJ):
                            last = product(ps[:, g * DUO:(g + 1) * DUO],
                                           (wqkvT_hi[:, j, cols], wqkvT_lo[:, j, cols]),
                                           (hT_hi[:, j, :], hT_lo[:, j, :]), j == 0, j == CJ - 1)
                    last.then_inc(act_filled, 1)

            def project_v(s):
                ps = dve_fill(s, "v")
                for i in range(2):
                    toks = slice(i * P, (i + 1) * P)
                    for j in range(CJ):
                        last = product(ps[:, i * C:(i + 1) * C], (hT_hi[:, j, toks], hT_lo[:, j, toks]),
                                       (wqkvT_hi[:, j, 2 * C:3 * C], wqkvT_lo[:, j, 2 * C:3 * C]), j == 0, j == CJ - 1)
                last.then_inc(dve_filled, 1)

            def features(s, w, tiles):
                if tiles[0] == 0:
                    pe.wait_ge(qk_split, s.at(lambda n: 2 * (n + 1) + w + 1))
                for j in tiles:
                    ps = act_fill(s, f"feat{w}{j}")
                    rows = slice(32 * j, 32 * j + 32)
                    for g in range(CJ):
                        last = product(ps[:, g * DUO:(g + 1) * DUO], (pbd_hi[rows, g, :], pbd_lo[rows, g, :]),
                                       (qkT_hi[rows, w, g, :], qkT_lo[rows, w, g, :]), True, True)
                    last.then_inc(act_filled, 1)

            def weights(s, i, r):
                fq, fk = feat
                toks = slice(i * P, (i + 1) * P)
                if i == 0 and r == 0:
                    pe.wait_ge(act_freed, s.at(lambda n: fill(act_fills, "feat03")(n - 1) + 1))
                banks = [dve_fill(s, f"aw{i}{2 * r + a}") for a in range(2)]
                for j in range(4):
                    last = []
                    for a in range(2):
                        rows = slice(a * M, (a + 1) * M)
                        last.append(nc.tensor.matmul(banks[a][:, j * P:(j + 1) * P], fk[rows, 4 * r + j, toks],
                                                     fq[rows, 4 * r + j, toks], start=True, stop=True))
                for a in range(2):
                    last[a].then_inc(dve_filled, 1)

            def transpose_keys(s, i):
                for half in range(2):
                    ps = act_fill(s, f"kp{i}{half}")
                    for j in range(4):
                        last = nc.tensor.transpose(ps[:, j * P:(j + 1) * P], feat[1][:, 4 * half + j, i * P:(i + 1) * P],
                                                   ident[:, :])
                    last.then_inc(act_filled, 1)

            def context(s, i):
                toks = slice(i * P, (i + 1) * P)
                first_chunk = s.n % DPB == 0 and i == 0
                va = vaug[:, s.n % 2, i, :, :, :].rearrange("p h q w -> p h (q w)")
                if i == 0:
                    pe.wait_ge(v_split, s.at(lambda n: n + 1))
                if s.n > 0 or i > 0:
                    pe.wait_ge(attn_ready, s.at(lambda n: 2 * n + i))
                if has_route(s.n) and i == 1:
                    pe.wait_ge(route_read, s.at(lambda n: n // DPB))
                if not first_chunk:
                    pe.wait_ge(kv_ready, s.at(lambda n: chunks_with_state(n, i - 1)))
                for pair in range(NPAIR):
                    ps = ctx_bank[pair // 4][:, 0:H // 2 * PARTS * VW].rearrange("p (h q w) -> p h q w", q=PARTS, w=VW)
                    at = 2 * (pair % 4)
                    if pair % 4 == 0:
                        pe.wait_ge(aw_split, s.at(lambda n: 2 * (2 * n + i) + pair // 4 + 1))
                    if not first_chunk:
                        nc.tensor.matmul(ps[:, at:at + 2, 0, :], feat[0][:, pair, toks],
                                         kvbd[:, pair, :].rearrange("p (a w) -> p a w", a=2),
                                         start=at == 0, stop=False, skip_group_check=True)
                    for a in range(2):
                        for q in range(PARTS):
                            last = nc.tensor.matmul(ps[:, at + a, :, :].rearrange("p q w -> p (q w)"),
                                                    aw[q][:, pair // 4, a, pair % 4, :], va[:, 2 * pair + a, :],
                                                    start=first_chunk and at + a + q == 0, stop=at + a + q == 7 + PARTS - 1,
                                                    skip_group_check=True)
                last.then_inc(ctx_filled, 1)

            def state(s, i):
                if is_last(s.n, i):
                    return
                first_chunk = s.n % DPB == 0 and i == 0
                if s.n > 0 or i > 0:
                    pe.wait_ge(kv_ready, s.at(lambda n: chunks_with_state(n, i) - 1))
                pe.wait_ge(kp_split, s.at(lambda n: chunks_with_state(n, i)))
                for pair in range(NPAIR):
                    for at, (q, v) in enumerate(PRODUCTS):
                        last = nc.tensor.matmul(kv_bank[:, pair * 2 * VW:(pair + 1) * 2 * VW],
                                                kp[q][:, pair // 4, pair % 4, :],
                                                vaug[:, s.n % 2, i, 2 * pair:2 * pair + 2, v, :],
                                                start=first_chunk and pair + at == 0,
                                                stop=pair == NPAIR - 1 and at == len(PRODUCTS) - 1, skip_group_check=True)
                last.then_inc(kv_filled, 1)

            def transpose_attn(s, i):
                ps = dve_fill(s, f"aT{i}")
                pe.wait_ge(attn_ready, s.at(lambda n: 2 * n + i + 1))
                for j in range(CJ):
                    last = nc.tensor.transpose(ps[:, j * P:(j + 1) * P], attn[:, j * P:(j + 1) * P], ident[:, :])
                last.then_inc(dve_filled, 1)

            def project_out(s, i):
                ps = dve_fill(s, f"o{i}")
                pe.wait_ge(dve_freed, s.at(lambda n: fill(dve_fills, f"aT{i}")(n) + 1))
                for j in range(CJ):
                    last = product(ps[:, 0:C], (aT_hi[:, j, :], aT_lo[:, j, :]), (woT_hi[:, j, :], woT_lo[:, j, :]),
                                   j == 0, j == CJ - 1)
                last.then_inc(dve_filled, 1)

            def route(s):
                pe.wait_ge(attn_ready, s.at(lambda n: 2 * n + 1) if has_attn(s.n) else 2 * s.n)
                pe.wait_ge(act_freed, s.at(lambda n: fill(act_fills, "x2T")(n) + 1))
                parts = [(j, d) for j in range(CJ) for d in range(DPB)]
                for at, (j, d) in enumerate(parts):
                    last = nc.tensor.matmul(ctx_bank[0][0:1, 0:E], hsum[:, j, d:d + 1], wr_sb[:, j, :],
                                            start=at == 0, stop=at == len(parts) - 1)
                last.then_inc(route_filled, 1)

            def up(s, q):
                if q == 0:
                    pe.wait_ge(hF_split, s.at(lambda n: n - FFN_LAG + 1))
                    if s.n % DPB == 1:
                        pe.wait_ge(w1_split, s.at(lambda n: n // DPB))
                ps = act_fill(s, f"up{q}")
                slot = (s.n - FFN_LAG) % DPB
                for a in range(2):
                    for j in range(CJ):
                        last = product(ps[:, a * DUO:(a + 1) * DUO], (w1_hi[:, j, 2 * q + a, :], w1_lo[:, j, 2 * q + a, :]),
                                       (hF_hi[:, slot, j, :], hF_lo[:, slot, j, :]), j == 0, j == CJ - 1)
                last.then_inc(act_filled, 1)

            def down(s, i, half):
                if i == 0:
                    pe.wait_ge(h1_split, s.at(lambda n: 4 * (n - FFN_LAG) + 2 * half + 2))
                    if s.n % DPB == 1 and half == 0:
                        pe.wait_ge(w2_split, s.at(lambda n: n // DPB))
                if half == 0:
                    down_bank[i] = dve_fill(s, f"down{i}")
                toks = slice(i * P, (i + 1) * P)
                for f in range(half * FC // 2, (half + 1) * FC // 2):
                    last = product(down_bank[i][:, 0:C], (h1_hi[:, f, toks], h1_lo[:, f, toks]),
                                   (w2_hi[:, f, :], w2_lo[:, f, :]), f == 0, f == FC - 1)
                if half == 1:
                    last.then_inc(dve_filled, 1)

            down_bank = [None, None]

            def step(s):
                n = s.n
                front, attn, ffn = has_front(n), has_attn(n), has_ffn(n)
                if front:
                    pe.wait_ge(xn_ready, s.at(lambda n: 2 * (n + 2)))
                    transpose_norm(s, "xT", xn)
                if attn:
                    weights(s, 0, 0)
                if ffn:
                    up(s, 0)
                if attn:
                    weights(s, 0, 1)
                if ffn:
                    up(s, 1)
                if attn:
                    transpose_keys(s, 0)
                if front:
                    project_qk(s)
                if attn:
                    context(s, 0)
                if front:
                    project_v(s)
                if attn:
                    weights(s, 1, 0)
                if ffn:
                    up(s, 2)
                if attn:
                    state(s, 0)
                if ffn:
                    up(s, 3)
                if has_ln2(n):
                    pe.wait_ge(xn2_ready, s.at(lambda n: 2 * n))
                    transpose_norm(s, "x2T", xn2)
                if has_route(n):
                    route(s)
                if attn:
                    transpose_attn(s, 0)
                    weights(s, 1, 1)
                    if not is_last(n, 1):
                        transpose_keys(s, 1)
                    project_out(s, 0)
                for half in range(2):
                    if ffn:
                        down(s, 0, half)
                    if front:
                        features(s, 1, (2 * half, 2 * half + 1))
                if attn:
                    context(s, 1)
                if front:
                    features(s, 0, (0, 1))
                if ffn:
                    down(s, 1, 0)
                if attn:
                    state(s, 1)
                    transpose_attn(s, 1)
                if front:
                    features(s, 0, (2, 3))
                if ffn:
                    down(s, 1, 1)
                if attn:
                    project_out(s, 1)

            pe.wait_ge(pbd_ready, 6)
            run(pe, step)


_INS = ["L0_attn_x", "L0_attn_Wqkv", "L0_attn_bqkv", "L0_attn_Wout", "L0_attn_bout", "L0_attn_proj", "L0_ffn_Wr",
        "L0_ffn_br", "L0_ffn_W1", "L0_ffn_b1", "L0_ffn_W2", "L0_ffn_b2", "L0_c", "L0_wmod"]


def kernel(**inputs):
    import numpy as _np
    import concourse.bacc as _bacc
    from concourse.bass_utils import run_bass_kernel_spmd as _run

    nc = _bacc.Bacc("TRN2", target_bir_lowering=False, num_devices=1)
    arrays, args = {}, []
    for name in _INS:
        a = _np.ascontiguousarray(inputs[name])
        arrays[f"in_{name}"] = a
        args.append(nc.dram_tensor(f"in_{name}", a.shape, mybir.dt.from_np(a.dtype), kind="ExternalInput").ap())
    args.append(nc.dram_tensor("out_0", (B, T, C), F32, kind="ExternalOutput").ap())
    program(nc, *args)
    return _run(nc, [arrays], core_ids=[0]).results[0]["out_0"]
```

```python
from contextlib import ExitStack

import concourse.bass as bass
from concourse import mybir

F32 = mybir.dt.float32
F32R = mybir.dt.float32r
BF16 = mybir.dt.bfloat16
U32 = mybir.dt.uint32
ALU = mybir.AluOpType
ACT = mybir.ActivationFunctionType

P = 128
B, T, C = 8, 1024, 256
H, D, M = 16, 16, 64
E, F = 8, 1024
NPAIR = H // 2
CJ = C // P
FC = F // P
DUO = 2 * P
DPB = T // DUO
ND = B * DPB
VW = D + 1
PARTS = 3
EPS = 1e-5
DELTA = 1e-6
FFN_LAG = 5
LOOP = range(9, 13)
TURNS = 5


class Step:

    def __init__(self, n, k=None):
        self.n, self.k = n, k

    def at(self, f):
        a = f(self.n)
        if self.k is None:
            return a
        slope = f(self.n + DPB) - a
        if slope == 0:
            return a
        assert f(self.n + 2 * DPB) - a == 2 * slope
        return self.k * slope + a


def has_front(n):
    return n + 1 < ND


def has_attn(n):
    return 0 <= n < ND


def has_ln2(n):
    return 1 <= n <= ND


def has_ffn(n):
    return FFN_LAG <= n < ND + FFN_LAG


def has_move(n):
    return DPB <= n < ND + DPB


def has_route(n):
    return n % DPB == 0 and DPB <= n <= ND


def is_last(n, i):
    return n % DPB == DPB - 1 and i == 1


def act_fills(n):
    out = []
    if has_front(n):
        out += ["xT"]
    if has_attn(n):
        out += ["kp00"]
    if has_ffn(n):
        out += ["up0"]
    if has_attn(n):
        out += ["kp01"]
    if has_ffn(n):
        out += ["up1"]
    if has_front(n):
        out += ["qk1"]
    if has_ffn(n):
        out += ["up2", "up3"]
    if has_ln2(n):
        out += ["x2T"]
    if has_attn(n) and not is_last(n, 1):
        out += ["kp10", "kp11"]
    if has_front(n):
        out += ["feat10", "feat11", "qk0", "feat12", "feat13"] + [f"feat0{j}" for j in range(4)]
    return out


def dve_fills(n):
    out = []
    if has_attn(n):
        out += ["aw00", "aw01", "aw02", "aw03", "aw10", "aw11", "aT0", "aw12", "aw13", "o0"]
    if has_ffn(n):
        out += ["down0"]
    if has_front(n):
        out += ["v"]
    if has_ffn(n):
        out += ["down1"]
    if has_attn(n):
        out += ["aT1", "o1"]
    return out


def fill(fills, name):
    return lambda n: sum(len(fills(m)) for m in range(-1, n)) + fills(n).index(name)


def chunks_with_state(n, i):
    return (n // DPB) * (2 * DPB - 1) + 2 * (n % DPB) + i + 1


def program(nc, x, wqkv, bqkv, wout, bout, proj, wr, br, w1, b1, w2, b2, c, wmod, out):
    with ExitStack() as ctx:
        ctx.enter_context(nc.allow_non_contiguous_dma(reason="small bias and condition loads"))

        def sb(name, shape, dt=F32):
            return ctx.enter_context(nc.sbuf_tensor(name, shape, dt))

        def pb(name):
            return ctx.enter_context(nc.psum_tensor(name, [P, 512], F32))

        def sem(name):
            return ctx.enter_context(nc.semaphore(name))

        ident = sb("ident", [P, P])
        mask = sb("mask", [P, P])
        wqkvT_hi = sb("wqkvT_hi", [P, CJ, 3 * C], F32R)
        wqkvT_lo = sb("wqkvT_lo", [P, CJ, 3 * C], F32R)
        woT_hi = sb("woT_hi", [P, CJ, C], F32R)
        woT_lo = sb("woT_lo", [P, CJ, C], F32R)
        pbd = sb("pbd", [P, CJ, P])
        pbd_hi = sb("pbd_hi", [P, CJ, P], F32R)
        pbd_lo = sb("pbd_lo", [P, CJ, P], F32R)
        bqk = sb("bqk", [P, 4])
        bv = sb("bv", [P, C])
        bo = sb("bo", [P, C])
        gbo = sb("gbo", [P, C])
        wr_sb = sb("wr_sb", [P, CJ, E])
        br_sb = sb("br_sb", [1, E])
        cT = sb("cT", [P, CJ, B])
        scT = sb("scT", [P, CJ, B])
        modT = sb("modT", [P, 4, CJ, B])
        ga = sb("ga", [P, C])
        gb = sb("gb", [P, C])

        xin = sb("xin", [P, DPB, 2, C])
        x1 = sb("x1", [P, DPB, 2, C])
        res = sb("res", [P, 2, 2, C])
        eps = sb("eps", [P, 1])
        stats = [sb(f"stats{q}", [P, 2, 6]) for q in range(2)]
        mv = [sb(f"mv{q}", [P, 2, 2]) for q in range(2)]
        std = [sb(f"std{q}", [P, 2]) for q in range(2)]
        rstd = [sb(f"rstd{q}", [P, 2]) for q in range(2)]
        xn = sb("xn", [P, 2, C])
        xn2 = sb("xn2", [P, 2, C])
        h_full = sb("h_full", [P, CJ, DUO])
        hT_hi = sb("hT_hi", [P, CJ, DUO], F32R)
        hT_lo = sb("hT_lo", [P, CJ, DUO], F32R)
        hF_hi = sb("hF_hi", [P, DPB, CJ, DUO], F32R)
        hF_lo = sb("hF_lo", [P, DPB, CJ, DUO], F32R)
        hsum = sb("hsum", [P, CJ, DPB])
        qkT = sb("qkT", [P, 2, CJ, DUO])
        qkT_hi = sb("qkT_hi", [P, 2, CJ, DUO], F32R)
        qkT_lo = sb("qkT_lo", [P, 2, CJ, DUO], F32R)
        feat = [sb(f"feat_{w}", [P, NPAIR, DUO]) for w in "qk"]
        kp = sb("kp", [P, NPAIR, P])
        vaug = sb("vaug", [P, 2, 2, H, VW])
        v_rest = sb("v_rest", [P, 2, H, D])
        v_parts = sb("v_parts", [P, 2, 2, H, PARTS, VW], BF16)
        aw_full = sb("aw_full", [P, 2, 2, 4, P])
        aw = [sb(f"aw{q}", [P, 2, 2, 4, P], BF16) for q in range(PARTS)]
        csum = sb("csum", [P, H, VW])
        kvbd = sb("kvbd", [P, NPAIR, 2 * VW])
        den = sb("den", [P, H])
        rden = sb("rden", [P, H])
        attn = sb("attn", [P, C])
        aT_hi = sb("aT_hi", [P, CJ, P], F32R)
        aT_lo = sb("aT_lo", [P, CJ, P], F32R)

        w1raw = sb("w1raw", [P, CJ, F])
        w1_hi = sb("w1_hi", [P, CJ, FC, P], F32R)
        w1_lo = sb("w1_lo", [P, CJ, FC, P], F32R)
        padded = [w1_hi[:, 0, :, :], w1_lo[:, 0, :, :]]
        w2raw = w1raw[:, :, :].rearrange("p j f -> p (j f)").rearrange("p (f c) -> p f c", c=C)
        w2raw_end = feat[0][:, :, :].rearrange("p a t -> p (a t)").rearrange("p (f c) -> p f c", c=C)
        w2_hi = sb("w2_hi", [P, FC, C], F32R)
        w2_lo = sb("w2_lo", [P, FC, C], F32R)
        b1_sb = sb("b1_sb", [P, FC])
        b2_sb = sb("b2_sb", [P, C])
        gb2 = sb("gb2", [P, C])
        y_gated = sb("y_gated", [P, C])
        h1 = sb("h1", [P, 2, 2, DUO])
        h1_hi = sb("h1_hi", [P, FC, DUO], F32R)
        h1_lo = sb("h1_lo", [P, FC, DUO], F32R)
        score = sb("score", [1, E])
        best = sb("best", [1, E])
        which = sb("which", [1, E], U32)

        wqkv_raw = feat[0][:, :, :].rearrange("p a t -> p (a t)")[:, 0:6 * C].rearrange("p (o c) -> p o c", c=C)
        wout_raw = feat[1][:, :, :].rearrange("p a t -> p (a t)")[:, 0:2 * C].rearrange("p (o c) -> p o c", c=C)
        wmod_a = w1raw[:, :, :]
        wmod_b = h1[:, :, :, :].rearrange("p a b t -> p (a b t)").rearrange("p (j n) -> p j n", j=CJ)
        gate_raw, gate_abs = (aw_full[0:B, 0, q, :, :].rearrange("p j t -> p (j t)").rearrange("p (g c) -> p g c", g=2)
                              for q in range(2))
        gate_row = xn2[0:B, :, :]

        gates_dram = nc.dram_tensor("gates_dram", (B, 2, C), F32, kind="Internal").ap()

        act_bank = [pb("act_bank0"), pb("act_bank1")]
        dve_bank = [pb("dve_bank0"), pb("dve_bank1"), pb("dve_bank2")]
        ctx_bank = [pb("ctx_low"), pb("ctx_high")]
        kv_bank = pb("kv_bank")

        s_wqkv, s_wout, s_small, s_pbd = sem("s_wqkv"), sem("s_wout"), sem("s_small"), sem("s_pbd")
        s_cond, s_wmod_first, s_wmod_rest = sem("s_cond"), sem("s_wmod_first"), sem("s_wmod_rest")
        zeroed, consts_ready = sem("zeroed"), sem("consts_ready")
        silu_ready = sem("silu_ready")
        setup_filled, setup_freed = sem("setup_filled"), sem("setup_freed")
        mod_filled, mod_ready = sem("mod_filled"), sem("mod_ready")
        gate_chain, gates_stored = sem("gate_chain"), sem("gates_stored")
        pbd_ready, padded_ready = sem("pbd_ready"), sem("padded_ready")
        x_loaded = sem("x_loaded")
        ga_loaded, gb_loaded = sem("ga_loaded"), sem("gb_loaded")
        w1_loaded, w2_loaded, b1_loaded, b2_loaded = sem("w1_loaded"), sem("w2_loaded"), sem("b1_loaded"), sem("b2_loaded")
        out_stored = sem("out_stored")
        act_filled, act_freed = sem("act_filled"), sem("act_freed")
        dve_filled, dve_freed = sem("dve_filled"), sem("dve_freed")
        aw_first, aw_rest, aw_second, aw_split = sem("aw_first"), sem("aw_rest"), sem("aw_second"), sem("aw_split")
        v_copied, v_rest_ready, v_split = sem("v_copied"), sem("v_rest_ready"), sem("v_split")
        route_filled, route_read = sem("route_filled"), sem("route_read")
        ctx_filled, attn_ready = sem("ctx_filled"), sem("attn_ready")
        kv_filled, kv_ready = sem("kv_filled"), sem("kv_ready")
        stats_chain = [sem("stats_chain0"), sem("stats_chain1")]
        std_ready = [sem("std_ready0"), sem("std_ready1")]
        rstd_ready = [sem("rstd_ready0"), sem("rstd_ready1")]
        xn_ready, xn2_ready = sem("xn_ready"), sem("xn2_ready")
        hT_split, hF_split, qk_split = sem("hT_split"), sem("hF_split"), sem("qk_split")
        norm_chain, aT_hi_ready = sem("norm_chain"), sem("aT_hi_ready")
        gbo_ready, gb2_ready = sem("gbo_ready"), sem("gb2_ready")
        x1_ready, result_ready = sem("x1_ready"), sem("result_ready")
        xb_ready, res_copied, x2_ready = sem("xb_ready"), sem("res_copied"), sem("x2_ready")
        score_chain, expert_ready = sem("score_chain"), sem("expert_ready")
        w1_hi_ready, w1_split = sem("w1_hi_ready"), sem("w1_split")
        w2_hi_ready, w2_split = sem("w2_hi_ready"), sem("w2_split")
        h1_split = sem("h1_split")

        x_v = x.rearrange("b (d i p) c -> p (b d) i c", i=2, p=P)
        out_v = out.rearrange("b (d i p) c -> p (b d) i c", i=2, p=P)
        gates_v = gates_dram.rearrange("b g c -> g b c")

        block = ctx.enter_context(nc.Block())

        def run(eng, step):
            for n in range(-1, LOOP[0]):
                step(Step(n))
            with eng.Fori(0, TURNS) as k:
                for n in LOOP:
                    step(Step(n, k))
            for n in range(LOOP[0] + DPB * TURNS, ND + FFN_LAG):
                step(Step(n))

        def wait_apart(eng, of, count):
            count = eng.to_reg(count) if not isinstance(count, int) else count
            eng.wait_ge(consts_ready, 1)
            eng.wait_ge(of, count)

        @block.sync
        def _(sp):
            sp.dma_start(xin[:, 0, :, :], x_v[:, 0, :, :]).then_inc(x_loaded, 16)
            sp.dma_start(wqkv_raw, wqkv.rearrange("(o p) c -> p o c", p=P)).then_inc(s_wqkv, 16)
            sp.wait_ge(zeroed, 1)
            for h in range(H):
                sp.dma_start(pbd[(h % 8) * D:(h % 8 + 1) * D, h // 8, (h % 2) * M:(h % 2 + 1) * M], proj[h, :, :])\
                  .then_inc(s_pbd, 16)
            sp.dma_start(wout_raw, wout.rearrange("(o p) c -> p o c", p=P)).then_inc(s_wout, 16)
            for m in (1, 2):
                sp.wait_ge(x_loaded, 16 * m)
                sp.dma_start(xin[:, m, :, :], x_v[:, m, :, :]).then_inc(x_loaded, 16)
            sp.wait_ge(gate_chain, 3)
            sp.dma_start(gates_dram, gate_row[:, :, :]).then_inc(gates_stored, 16)
            sp.wait_ge(gates_stored, 16)
            sp.dma_start(ga[:, :], gates_v[0, 0:1, :].to_broadcast([P, C])).then_inc(ga_loaded, 16)

            def step(s):
                n = s.n
                if 0 <= n and n + 3 < ND:
                    if n >= 1:
                        wait_apart(sp, xn2_ready, s.at(lambda n: 2 * n))
                    wait_apart(sp, x_loaded, s.at(lambda n: 16 * (n + 3)))
                    sp.dma_start(xin[:, (n + 3) % DPB, :, :],
                                 x_v[:, bass.ds(s.at(lambda n: n + 3), 1), :, :].rearrange("p m i c -> p (m i) c"))\
                      .then_inc(x_loaded, 16)
                if has_route(n):
                    wait_apart(sp, expert_ready, s.at(lambda n: n // DPB))
                    expert = sp.value_load(which[0:1, 0:1], min_val=0, max_val=E - 1)
                    if n > DPB:
                        wait_apart(sp, w2_split, s.at(lambda n: 2 * (n // DPB - 1)))
                        wait_apart(sp, h1_split, s.at(lambda n: 4 * (n - FFN_LAG + 1)))
                    sp.dma_start(w1raw[:, :, :], w1[bass.ds(expert, 1), :, :].rearrange("e (j p) f -> p (e j) f", p=P))\
                      .then_inc(w1_loaded, 16)
                    sp.dma_start(b1_sb[:, :], b1[bass.ds(expert, 1), :].rearrange("e (p f) -> p (e f)", p=P))\
                      .then_inc(b1_loaded, 16)
                    if n < ND:
                        wait_apart(sp, w1_split, s.at(lambda n: 2 * (n // DPB)))
                    sp.dma_start((w2raw if n < ND else w2raw_end)[:, :, :], w2[bass.ds(expert, 1), :, :].rearrange("e (p f) c -> p (e f) c", p=P))\
                      .then_inc(w2_loaded, 16)
                    sp.dma_start(b2_sb[:, :], b2[bass.ds(expert, 1), :].to_broadcast([P, C])).then_inc(b2_loaded, 16)
                if has_ffn(n):
                    if n > FFN_LAG:
                        wait_apart(sp, out_stored, s.at(lambda n: 16 * (n - FFN_LAG)))
                    wait_apart(sp, result_ready, s.at(lambda n: 2 * (n - FFN_LAG + 1)))
                    sp.dma_start(out_v[:, bass.ds(s.at(lambda n: n - FFN_LAG), 1), :, :]
                                 .rearrange("p m i c -> p (m i) c"), res[:, (n - FFN_LAG) % 2, :, :])\
                      .then_inc(out_stored, 16)
                if has_route(n):
                    sp.dma_start(gb[:, :], gates_v[1, bass.ds(s.at(lambda n: n // DPB - 1), 1), :].to_broadcast([P, C]))\
                      .then_inc(gb_loaded, 16)
                if n % DPB == DPB - 1 and 0 <= n < ND - 1:
                    wait_apart(sp, x1_ready, s.at(lambda n: 2 * n + 2))
                    sp.dma_start(ga[:, :], gates_v[0, bass.ds(s.at(lambda n: n // DPB + 1), 1), :].to_broadcast([P, C]))\
                      .then_inc(ga_loaded, 16)

            run(sp, step)
            sp.wait_ge(out_stored, 16 * ND)

        @block.scalar
        def _(act):
            wmod_v = wmod.rearrange("(j p) n -> p j n", p=P)
            for j in range(CJ):
                act.dma_start(cT[:, j, :], c[:, j * P:(j + 1) * P].rearrange("b p -> p b")).then_inc(s_cond, 16)
            act.dma_start(wmod_a[:, :, 0:2 * C], wmod_v[:, :, 0:2 * C]).then_inc(s_wmod_first, 16)
            act.dma_start(bqk[:, :], bqkv[0:2 * C].rearrange("(o p) -> p o", p=P)).then_inc(s_small, 16)
            act.dma_start(bv[:, :], bqkv[2 * C:3 * C].rearrange("(a c) -> a c", a=1).to_broadcast([P, C])).then_inc(s_small, 16)
            act.dma_start(wmod_a[:, :, 2 * C:1024], wmod_v[:, :, 2 * C:1024]).then_inc(s_wmod_rest, 16)
            act.dma_start(wmod_b, wmod_v[:, :, 1024:1536]).then_inc(s_wmod_rest, 16)
            act.dma_start(bo[:, :], bout.rearrange("(a c) -> a c", a=1).to_broadcast([P, C])).then_inc(s_small, 16)
            act.dma_start(wr_sb[:, :, :], wr.rearrange("(j p) e -> p j e", p=P)).then_inc(s_small, 16)
            act.dma_start(br_sb[:, :], br.rearrange("(a e) -> a e", a=1)).then_inc(s_small, 16)
            def drain(s, name):
                if name in ("xT", "x2T"):
                    wait_apart(act, act_filled, s.at(lambda n: fill(act_fills, name)(n) + 1))
                else:
                    act.wait_ge(act_filled, s.at(lambda n: fill(act_fills, name)(n) + 1))
                return act_bank[fill(act_fills, name)(s.n) % 2]

            def kp_copy(s, i, half):
                ps = drain(s, f"kp{i}{half}")
                if half == 0 and (s.n > 0 or i > 0):
                    act.wait_ge(kv_filled, s.at(lambda n: chunks_with_state(n, i) - 1))
                nc.scalar.activation(kp[:, 4 * half:4 * half + 4, :], ps[:, :].rearrange("p (a s) -> p a s", s=P),
                                     ACT.Copy).then_inc(act_freed, 1)

            def second_weights(s, i, r):
                act.wait_ge(aw_rest, s.at(lambda n: 2 * (2 * n + i) + r + 1))
                nc.scalar.activation(aw[1][:, r, :, :, :], aw_full[:, r, :, :, :], ACT.Copy).then_inc(aw_second, 1)

            def first_values(s):
                act.wait_ge(dve_freed, s.at(lambda n: fill(dve_fills, "v")(n) + 1))
                nc.scalar.activation(v_parts[:, (s.n + 1) % 2, :, :, 0, 0:D], vaug[:, (s.n + 1) % 2, :, :, 0:D], ACT.Copy)\
                  .then_inc(v_copied, 1)

            def second_values(s):
                act.wait_ge(v_rest_ready, s.at(lambda n: n + 2))
                nc.scalar.activation(v_parts[:, (s.n + 1) % 2, :, :, 1, 0:D], v_rest[:, :, :, :], ACT.Copy)\
                  .then_inc(v_copied, 1)

            def modulate(s, ps, full, hi, shift, gain, batch, sums):
                for j in range(CJ):
                    src = ps[:, j * DUO:(j + 1) * DUO]
                    scale = modT[:, gain, j, bass.ds(batch, 1)]
                    bias = modT[:, shift, j, bass.ds(batch, 1)]
                    nc.scalar.activation(full[:, j, :], src, ACT.Identity, bias=bias, scale=scale,
                                         accum_out=None if sums is None else sums[:, j:j + 1])
                    last = nc.scalar.activation(hi[:, j, :], src, ACT.Identity, bias=bias, scale=scale)
                return last

            def state_copy(s, i):
                act.wait_ge(kv_filled, s.at(lambda n: chunks_with_state(n, i)))
                ps = kv_bank[:, 0:NPAIR * 2 * VW].rearrange("p (a w) -> p a w", w=2 * VW)
                nc.scalar.activation(kvbd[0:M, :, 0:VW], ps[0:M, :, 0:VW], ACT.Copy)
                nc.scalar.activation(kvbd[M:P, :, VW:2 * VW], ps[M:P, :, VW:2 * VW], ACT.Copy).then_inc(kv_ready, 1)

            def queries_or_keys(s, w):
                ps = drain(s, f"qk{w}")
                if s.n >= 0:
                    act.wait_ge(qk_split, s.at(lambda n: 2 * (n + 1)))
                for g in range(CJ):
                    src = ps[:, g * DUO:(g + 1) * DUO]
                    bias = bqk[:, 2 * w + g:2 * w + g + 1]
                    nc.scalar.activation(qkT[:, w, g, :], src, ACT.Identity, bias=bias)
                    last = nc.scalar.activation(qkT_hi[:, w, g, :], src, ACT.Identity, bias=bias)
                last.then_inc(act_freed, 1)

            def features(s, w, tiles):
                dst = feat[w][:, :, :].rearrange("p (g j) t -> p g j t", j=4)
                for j in tiles:
                    ps = drain(s, f"feat{w}{j}")
                    nc.scalar.activation(dst[:, :, j, :], ps[:, :].rearrange("p (g t) -> p g t", t=DUO), ACT.Relu)\
                      .then_inc(act_freed, 1)

            def deviation(s, q, duo):
                act.wait_ge(stats_chain[q], s.at(lambda n: 4 * duo(n) + 4))
                nc.scalar.activation(std[q][:, :], mv[q][:, :, 1], ACT.Sqrt, bias=eps[:, :]).then_inc(std_ready[q], 1)

            def up(s, q):
                if s.n % DPB == 1 and q == 0:
                    act.wait_ge(b1_loaded, s.at(lambda n: 16 * (n // DPB)))
                ps = drain(s, f"up{q}")
                if s.n > FFN_LAG or q >= 2:
                    act.wait_ge(h1_split, s.at(lambda n: 4 * (n - FFN_LAG) + q - 1))
                for a in range(2):
                    src = ps[:, a * DUO:(a + 1) * DUO]
                    bias = b1_sb[:, 2 * q + a:2 * q + a + 1]
                    nc.scalar.activation(h1[:, q % 2, a, :], src, ACT.Relu, bias=bias)
                    last = nc.scalar.activation(h1_hi[:, 2 * q + a, :], src, ACT.Relu, bias=bias)
                last.then_inc(act_freed, 1)

            def step(s):
                n = s.n
                if n == -1:
                    act.wait_ge(s_cond, 16 * CJ)
                    nc.scalar.activation(scT[:, :, :], cT[:, :, :], ACT.Silu).then_inc(silu_ready, 1)
                    act.wait_ge(zeroed, 9)
                    deviation(Step(-2), 0, lambda n: n + 2)
                if has_front(n):
                    ps = drain(s, "xT")
                    if n == -1:
                        act.wait_ge(mod_ready, 2)
                    if n >= 2:
                        wait_apart(act, hF_split, s.at(lambda n: n - 1))
                    elif n >= 0:
                        wait_apart(act, hT_split, n + 1)
                    modulate(s, ps, h_full, hT_hi, 0, 1, s.at(lambda n: (n + 1) // DPB), None).then_inc(act_freed, 1)
                if has_ln2(n):
                    deviation(s, 1, lambda n: n - 1)
                if has_attn(n):
                    kp_copy(s, 0, 0)
                if has_ffn(n):
                    up(s, 0)
                if has_attn(n):
                    second_weights(s, 0, 0)
                    kp_copy(s, 0, 1)
                if has_ffn(n):
                    up(s, 1)
                if has_attn(n):
                    second_weights(s, 0, 1)
                if has_front(n):
                    if n == -1:
                        act.wait_ge(s_small, 16 * 5)
                    queries_or_keys(s, 1)
                if has_move(n):
                    act.wait_ge(xn2_ready, s.at(lambda n: 2 * (n - DPB + 1)))
                    if n > FFN_LAG:
                        act.wait_ge(out_stored, s.at(lambda n: 16 * (n - FFN_LAG)))
                    nc.scalar.activation(res[:, (n - DPB) % 2, :, :], x1[:, (n - DPB) % DPB, :, :], ACT.Copy)\
                      .then_inc(res_copied, 1)
                if has_ffn(n) and n % DPB == 1:
                    act.wait_ge(w2_loaded, s.at(lambda n: 16 * (n // DPB)))
                    if n > FFN_LAG:
                        act.wait_ge(dve_freed, s.at(lambda n: fill(dve_fills, "down1")(n - 1) + 1))
                    nc.scalar.activation(w2_hi[:, :, :], (w2raw if n < ND else w2raw_end)[:, :, :], ACT.Copy).then_inc(w2_hi_ready, 1)
                if has_attn(n):
                    second_weights(s, 1, 0)
                if has_ffn(n):
                    up(s, 2)
                if has_attn(n):
                    state_copy(s, 0)
                if has_ffn(n):
                    up(s, 3)
                if has_ln2(n):
                    ps = drain(s, "x2T")
                    if n == 1:
                        act.wait_ge(mod_ready, 4)
                    if has_front(n):
                        wait_apart(act, hT_split, s.at(lambda n: n + 2))
                    else:
                        wait_apart(act, hF_split, n - 1)
                    slot = (n - 1) % DPB
                    modulate(s, ps, h_full, hF_hi[:, slot, :, :], 2, 3, s.at(lambda n: (n - 1) // DPB),
                             hsum[:, :, slot]).then_inc(act_freed, 1)
                if n + 2 < ND:
                    deviation(s, 0, lambda n: n + 2)
                if has_attn(n) and not is_last(n, 1):
                    kp_copy(s, 1, 0)
                    kp_copy(s, 1, 1)
                if has_attn(n):
                    second_weights(s, 1, 1)
                if has_front(n):
                    features(s, 1, (0, 1))
                    queries_or_keys(s, 0)
                    features(s, 1, (2, 3))
                if has_route(n):
                    act.wait_ge(w1_loaded, s.at(lambda n: 16 * (n // DPB)))
                    for j in range(CJ):
                        nc.scalar.activation(w1_hi[:, j, :, :], w1raw[:, j, :].rearrange("p (q f) -> p f q", f=FC),
                                             ACT.Copy).then_inc(w1_hi_ready, 1)
                if has_front(n):
                    first_values(s)
                    features(s, 0, range(4))
                if has_attn(n) and not is_last(n, 1):
                    state_copy(s, 1)
                if has_front(n):
                    second_values(s)

            run(act, step)

        @block.gpsimd
        def _(pool):
            nc.gpsimd.memset(pbd[:, :, :], 0.0).then_inc(zeroed, 1)
            nc.gpsimd.memset(ident[:, :], 0.0).then_inc(zeroed, 1)
            nc.gpsimd.memset(mask[:, :], 1.0).then_inc(zeroed, 1)
            nc.gpsimd.memset(vaug[:, :, :, :, D:VW], 1.0).then_inc(zeroed, 1)
            nc.gpsimd.memset(v_parts[:, :, :, :, 0, D:VW], 1.0).then_inc(zeroed, 1)
            nc.gpsimd.memset(v_parts[:, :, :, :, 1:PARTS, D:VW], 0.0).then_inc(zeroed, 1)
            nc.gpsimd.memset(kvbd[:, :, :], 0.0).then_inc(zeroed, 1)
            nc.gpsimd.memset(eps[:, :], EPS).then_inc(zeroed, 1)
            nc.gpsimd.memset(qkT[:, :, :, :], 0.0).then_inc(zeroed, 1)
            pool.wait_ge(zeroed, 9)
            nc.gpsimd.affine_select(out=ident[:, :], in_=ident[:, :], compare_op=ALU.not_equal, fill=1.0, base=0,
                                    pattern=[[-1, P]], channel_multiplier=1).then_inc(consts_ready, 1)
            nc.gpsimd.affine_select(out=mask[:, :], in_=mask[:, :], compare_op=ALU.is_ge, fill=0.0, base=0,
                                    pattern=[[1, P]], channel_multiplier=-1).then_inc(consts_ready, 1)

            def minus_hi(lo, full, hi):
                return nc.gpsimd.tensor_tensor(lo, full, hi.bitcast(F32), ALU.subtract)

            def third_weights(s, i, r):
                pool.wait_ge(aw_second, s.at(lambda n: 2 * (2 * n + i) + r + 1))
                nc.gpsimd.tensor_tensor(aw[2][:, r, :, :, :], aw_full[:, r, :, :, :], aw[1][:, r, :, :, :], ALU.subtract)\
                  .then_inc(aw_split, 1)

            def qk_lower(s, w):
                pool.wait_ge(act_freed, s.at(lambda n: fill(act_fills, f"qk{w}")(n) + 1))
                minus_hi(qkT_lo[:, w, :, :], qkT[:, w, :, :], qkT_hi[:, w, :, :]).then_inc(qk_split, 1)

            def h1_lower(s, q):
                pool.wait_ge(act_freed, s.at(lambda n: fill(act_fills, f"up{q}")(n) + 1))
                minus_hi(h1_lo[:, 2 * q:2 * q + 2, :], h1[:, q % 2, :, :], h1_hi[:, 2 * q:2 * q + 2, :]).then_inc(h1_split, 1)

            def step(s):
                n = s.n
                if has_front(n):
                    pool.wait_ge(act_freed, s.at(lambda n: fill(act_fills, "xT")(n) + 1))
                    minus_hi(hT_lo[:, :, :], h_full[:, :, :], hT_hi[:, :, :]).then_inc(hT_split, 1)
                if has_attn(n) and n % DPB == 0:
                    if n == 0:
                        pool.wait_ge(s_small, 16 * 5)
                    else:
                        pool.wait_ge(xb_ready, s.at(lambda n: 2 * n))
                    pool.wait_ge(ga_loaded, s.at(lambda n: 16 * (n // DPB + 1)))
                    nc.gpsimd.tensor_tensor(gbo[:, :], bo[:, :], ga[:, :], ALU.mult).then_inc(gbo_ready, 1)
                if has_ffn(n):
                    if n % DPB == 1:
                        if n > FFN_LAG:
                            pool.wait_ge(x2_ready, s.at(lambda n: 2 * (n - FFN_LAG)))
                        pool.wait_ge(b2_loaded, s.at(lambda n: 16 * (n // DPB)))
                        pool.wait_ge(gb_loaded, s.at(lambda n: 16 * (n // DPB)))
                        nc.gpsimd.tensor_tensor(gb2[:, :], b2_sb[:, :], gb[:, :], ALU.mult).then_inc(gb2_ready, 1)
                        pool.wait_ge(gb2_ready, s.at(lambda n: n // DPB))
                    slot = (n - FFN_LAG) % 2
                    pool.wait_ge(res_copied, s.at(lambda n: n - FFN_LAG + 1))
                    for i in range(2):
                        nc.gpsimd.tensor_tensor(res[:, slot, i, :], res[:, slot, i, :], gb2[:, :], ALU.add)\
                          .then_inc(x2_ready, 1)
                if has_ffn(n):
                    h1_lower(s, 0)
                if has_attn(n):
                    third_weights(s, 0, 0)
                if has_ffn(n):
                    h1_lower(s, 1)
                if has_attn(n):
                    third_weights(s, 0, 1)
                    pool.wait_ge(xn_ready, s.at(lambda n: 2 * (n + 1)))
                    if n % DPB == 0:
                        pool.wait_ge(gbo_ready, s.at(lambda n: n // DPB + 1))
                    for i in range(2):
                        nc.gpsimd.tensor_tensor(xin[:, n % DPB, i, :], xin[:, n % DPB, i, :], gbo[:, :], ALU.add)\
                          .then_inc(xb_ready, 1)
                if has_front(n):
                    qk_lower(s, 1)
                if has_attn(n):
                    third_weights(s, 1, 0)
                if has_ffn(n):
                    if n % DPB == 1:
                        pool.wait_ge(w2_hi_ready, s.at(lambda n: n // DPB))
                        minus_hi(w2_lo[:, 0:4, :], (w2raw if n < ND else w2raw_end)[:, 0:4, :], w2_hi[:, 0:4, :]).then_inc(w2_split, 1)
                    h1_lower(s, 2)
                    h1_lower(s, 3)
                if has_ln2(n):
                    pool.wait_ge(act_freed, s.at(lambda n: fill(act_fills, "x2T")(n) + 1))
                    slot = (n - 1) % DPB
                    minus_hi(hF_lo[:, slot, :, :], h_full[:, :, :], hF_hi[:, slot, :, :]).then_inc(hF_split, 1)
                if has_attn(n):
                    third_weights(s, 1, 1)
                if has_front(n):
                    qk_lower(s, 0)
                    now = (n + 1) % 2
                    pool.wait_ge(v_copied, s.at(lambda n: 2 * (n + 1) + 1))
                    nc.gpsimd.tensor_tensor(v_rest[:, :, :, :], vaug[:, now, :, :, 0:D], v_parts[:, now, :, :, 0, 0:D],
                                            ALU.subtract).then_inc(v_rest_ready, 1)
                if has_route(n):
                    pool.wait_ge(w1_hi_ready, s.at(lambda n: 2 * (n // DPB) - 1))
                    minus_hi(w1_lo[:, 0, :, :], w1raw[:, 0, :].rearrange("p (q f) -> p f q", f=FC), w1_hi[:, 0, :, :])\
                      .then_inc(w1_split, 1)
                if has_front(n):
                    pool.wait_ge(v_copied, s.at(lambda n: 2 * (n + 1) + 2))
                    nc.gpsimd.tensor_tensor(v_parts[:, now, :, :, 2, 0:D], v_rest[:, :, :, :],
                                            v_parts[:, now, :, :, 1, 0:D], ALU.subtract).then_inc(v_split, 1)

            run(pool, step)

        @block.vector
        def _(dve):
            def drain(s, name):
                dve.wait_ge(dve_filled, s.at(lambda n: fill(dve_fills, name)(n) + 1))
                return dve_bank[fill(dve_fills, name)(s.n) % 3]

            def measure(s, q, i, src, duo):
                nc.vector.bn_stats(stats[q][:, i, :], src).then_inc(stats_chain[q], 1)
                wait_apart(dve, stats_chain[q], s.at(lambda n: 4 * duo(n) + 2 * i + 1))
                nc.vector.bn_aggr(mv[q][:, i, :], stats[q][:, i, :]).then_inc(stats_chain[q], 1)

            def apply_norm(s, q, src, dst, duo, done):
                dve.wait_ge(std_ready[q], s.at(lambda n: duo(n) + 1))
                nc.vector.reciprocal(rstd[q][:, :], std[q][:, :]).then_inc(rstd_ready[q], 1)
                dve.wait_ge(rstd_ready[q], s.at(lambda n: duo(n) + 1))
                for i in range(2):
                    nc.vector.tensor_scalar(dst[:, i, :], src[:, i, :], mv[q][:, i, 0:1], rstd[q][:, i:i + 1],
                                            ALU.subtract, ALU.mult).then_inc(done, 1)

            def split_weight(f):
                dve.wait_ge(setup_filled, f + 1)
                if f < 3:
                    dst = slice(f * C, (f + 1) * C)
                    hi, lo = wqkvT_hi[:, :, dst], wqkvT_lo[:, :, dst]
                else:
                    hi, lo = woT_hi[:, :, :], woT_lo[:, :, :]
                src = dve_bank[f % 2][:, :].rearrange("p (j o) -> p j o", j=CJ)
                nc.vector.tensor_copy(hi, src).then_inc(pbd_ready, 1)
                dve.wait_ge(pbd_ready, f + 1 if f < 3 else 6)
                nc.vector.tensor_tensor(lo, src, hi.bitcast(F32), ALU.subtract).then_inc(setup_freed, 1)

            def modulation(norm):
                dve.wait_ge(mod_filled, norm + 1)
                ps = ctx_bank[norm][:, 0:2 * CJ * B].rearrange("p (q j b) -> p q j b", q=2, j=CJ)
                for q in range(2):
                    nc.vector.tensor_scalar(modT[:, 2 * norm + q, :, :], ps[:, q, :, :], float(q), None, ALU.add)\
                      .then_inc(mod_ready, 1)

            def measure_first(s):
                dve.wait_ge(x_loaded, s.at(lambda n: 16 * (n + 3)))
                for i in range(2):
                    measure(s, 0, i, xin[:, (s.n + 2) % DPB, i, :], lambda n: n + 2)

            def apply_first(s):
                if s.n >= -1:
                    dve.wait_ge(act_filled, s.at(lambda n: fill(act_fills, "xT")(n) + 1))
                apply_norm(s, 0, xin[:, (s.n + 2) % DPB, :, :], xn, lambda n: n + 2, xn_ready)

            def mask_weights(s, i, r):
                if s.n > 0 or i > 0:
                    dve.wait_ge(aw_split, s.at(lambda n: 2 * (2 * n + i - 1) + r + 1))
                for a in range(2):
                    ps = drain(s, f"aw{i}{2 * r + a}")
                    nc.vector.tensor_tensor(aw_full[:, r, a, :, :], ps[:, :].rearrange("p (j t) -> p j t", t=P),
                                            mask[:, :].rearrange("p (a t) -> p a t", a=1).to_broadcast([P, 4, P]),
                                            ALU.mult).then_inc(dve_freed, 1)

            def split_weights(s, i, r):
                if s.n > 0 or i > 0:
                    dve.wait_ge(ctx_filled, s.at(lambda n: 2 * (2 * n + i - 1) + r + 1))
                dve.wait_ge(dve_freed, s.at(lambda n: fill(dve_fills, f"aw{i}{2 * r + 1}")(n) + 1))
                nc.vector.tensor_copy(aw[0][:, r, :, :, :], aw_full[:, r, :, :, :]).then_inc(aw_first, 1)
                dve.wait_ge(aw_first, s.at(lambda n: 2 * (2 * n + i) + r + 1))
                nc.vector.tensor_tensor(aw_full[:, r, :, :, :], aw_full[:, r, :, :, :], aw[0][:, r, :, :, :], ALU.subtract)\
                  .then_inc(aw_rest, 1)

            def add_value_bias(s):
                ps = drain(s, "v")
                nc.vector.tensor_tensor(
                    vaug[:, (s.n + 1) % 2, :, :, 0:D], ps[:, :].rearrange("p (i h d) -> p i h d", i=2, d=D),
                    bv[:, :].rearrange("p (a h d) -> p a h d", a=1, d=D).to_broadcast([P, 2, H, D]),
                    ALU.add).then_inc(dve_freed, 1)

            def normalise(s, i):
                if s.n > 0 or i > 0:
                    dve.wait_ge(attn_ready, s.at(lambda n: 2 * n + i))
                for b in range(2):
                    dve.wait_ge(ctx_filled, s.at(lambda n: 2 * (2 * n + i) + b + 1))
                    ps = ctx_bank[b][:, 0:H // 2 * PARTS * VW].rearrange("p (h q w) -> p h w q", q=PARTS, w=VW)
                    nc.vector.tensor_reduce(csum[:, b * H // 2:(b + 1) * H // 2, :], ps, mybir.AxisListType.X, ALU.add)\
                      .then_inc(norm_chain, 1)
                dve.wait_ge(norm_chain, s.at(lambda n: 4 * (2 * n + i) + 2))
                nc.vector.tensor_scalar(den[:, :], csum[:, :, D], DELTA, None, ALU.add).then_inc(norm_chain, 1)
                dve.wait_ge(norm_chain, s.at(lambda n: 4 * (2 * n + i) + 3))
                nc.vector.reciprocal(rden[:, :], den[:, :]).then_inc(norm_chain, 1)
                dve.wait_ge(norm_chain, s.at(lambda n: 4 * (2 * n + i) + 4))
                nc.vector.tensor_tensor(attn[:, :].rearrange("p (h d) -> p h d", d=D), csum[:, :, 0:D],
                                        rden[:, :].rearrange("p (h a) -> p h a", a=1).to_broadcast([P, H, D]),
                                        ALU.mult).then_inc(attn_ready, 1)

            def split_attn(s, i):
                ps = drain(s, f"aT{i}")
                src = ps[:, 0:C].rearrange("p (j t) -> p j t", t=P)
                nc.vector.tensor_copy(aT_hi[:, :, :], src).then_inc(aT_hi_ready, 1)
                dve.wait_ge(aT_hi_ready, s.at(lambda n: 2 * n + i + 1))
                nc.vector.tensor_tensor(aT_lo[:, :, :], src, aT_hi[:, :, :].bitcast(F32), ALU.subtract).then_inc(dve_freed, 1)

            def residual(s, i):
                ps = drain(s, f"o{i}")
                slot = s.n % DPB
                dve.wait_ge(xb_ready, s.at(lambda n: 2 * n + i + 1))
                if has_move(s.n) and i == 0:
                    dve.wait_ge(res_copied, s.at(lambda n: n - DPB + 1))
                if s.n % DPB == 0 and i == 0:
                    dve.wait_ge(ga_loaded, s.at(lambda n: 16 * (n // DPB + 1)))
                nc.vector.tensor_tensor(x1[:, slot, i, :], ps[:, 0:C], ga[:, :], ALU.mult).then_inc(dve_freed, 1)
                dve.wait_ge(dve_freed, s.at(lambda n: fill(dve_fills, f"o{i}")(n) + 1))
                nc.vector.tensor_tensor(x1[:, slot, i, :], x1[:, slot, i, :], xin[:, slot, i, :], ALU.add)\
                  .then_inc(x1_ready, 1)
                dve.wait_ge(x1_ready, s.at(lambda n: 2 * n + i + 1))
                measure(s, 1, i, x1[:, slot, i, :], lambda n: n)

            def finish(s, i):
                done = lambda n: 2 * (n - FFN_LAG) + i
                slot = (s.n - FFN_LAG) % 2
                if s.n % DPB == 1 and i == 0:
                    dve.wait_ge(gb_loaded, s.at(lambda n: 16 * (n // DPB)))
                if s.n > FFN_LAG or i > 0:
                    dve.wait_ge(result_ready, s.at(done))
                ps = drain(s, f"down{i}")
                nc.vector.tensor_tensor(y_gated[:, :], ps[:, 0:C], gb[:, :], ALU.mult).then_inc(dve_freed, 1)
                dve.wait_ge(x2_ready, s.at(lambda n: done(n) + 1))
                dve.wait_ge(dve_freed, s.at(lambda n: fill(dve_fills, f"down{i}")(n) + 1))
                nc.vector.tensor_tensor(res[:, slot, i, :], y_gated[:, :], res[:, slot, i, :], ALU.add)\
                  .then_inc(result_ready, 1)

            def route(s):
                dve.wait_ge(route_filled, s.at(lambda n: n // DPB))
                nc.vector.scalar_tensor_tensor(score[:, :], ctx_bank[0][0:1, 0:E], 1.0 / T, br_sb[:, :], ALU.mult, ALU.add)\
                  .then_inc(route_read, 1)
                wait_apart(dve, route_read, s.at(lambda n: n // DPB))
                nc.vector.max(best[:, :], score[:, :]).then_inc(score_chain, 1)
                wait_apart(dve, score_chain, s.at(lambda n: n // DPB))
                nc.vector.max_index(which[:, :], best[:, :], score[:, :]).then_inc(expert_ready, 1)

            dve.wait_ge(zeroed, 9)
            for part in padded:
                nc.vector.tensor_copy(part.rearrange("p a m -> p (a m)"), qkT[:, :, :, :].rearrange("p w g t -> p (w g t)"))\
                  .then_inc(padded_ready, 1)
            measure_first(Step(-2))
            for f in range(3):
                split_weight(f)
            apply_first(Step(-2))
            modulation(0)
            dve.wait_ge(s_pbd, 16 * H)
            dve.wait_ge(padded_ready, 2)
            nc.vector.tensor_copy(pbd_hi[:, :, :], pbd[:, :, :]).then_inc(pbd_ready, 1)
            dve.wait_ge(pbd_ready, 4)
            nc.vector.tensor_tensor(pbd_lo[:, :, :], pbd[:, :, :], pbd_hi[:, :, :].bitcast(F32), ALU.subtract)\
              .then_inc(pbd_ready, 1)
            split_weight(3)
            for part, src in zip(padded, (pbd_hi, pbd_lo)):
                for j in range(4):
                    rows = slice(32 * j, 32 * j + 32)
                    nc.vector.tensor_copy(part.rearrange("p (g j) m -> p g j m", j=4)[rows, :, j, :],
                                          src[rows, :, :].bitcast(F32)).then_inc(padded_ready, 1)
            modulation(1)
            dve.wait_ge(mod_filled, 3)
            nc.vector.tensor_copy(gate_raw[:, :, :], kv_bank[0:B, :].rearrange("p (q c) -> p q c", q=2)).then_inc(gate_chain, 1)
            dve.wait_ge(gate_chain, 1)
            nc.vector.scalar_tensor_tensor(gate_abs, gate_raw, -1.0, gate_raw, ALU.mult, ALU.max).then_inc(mod_ready, 1)
            dve.wait_ge(mod_ready, 5)
            nc.vector.tensor_scalar(gate_abs, gate_abs, 0.25, None, ALU.max).then_inc(mod_ready, 1)
            nc.vector.tensor_scalar(gate_row[:, :, :], gate_raw[:, :, :], 0.0, 2.0, ALU.is_ge, ALU.mult).then_inc(gate_chain, 1)
            dve.wait_ge(mod_ready, 6)
            dve.wait_ge(gate_chain, 2)
            nc.vector.scalar_tensor_tensor(gate_row[:, :, :], gate_row[:, :, :], -1.0, gate_abs[:, :, :],
                                           ALU.add, ALU.mult).then_inc(gate_chain, 1)
            dve.wait_ge(s_small, 16 * 5)

            def step(s):
                n = s.n
                if has_attn(n):
                    for r in range(2):
                        mask_weights(s, 0, r)
                        split_weights(s, 0, r)
                if has_ln2(n):
                    if n >= 2:
                        dve.wait_ge(act_filled, s.at(lambda n: fill(act_fills, "x2T")(n - 1) + 1))
                    apply_norm(s, 1, x1[:, (n - 1) % DPB, :, :], xn2, lambda n: n - 1, xn2_ready)
                if has_attn(n):
                    mask_weights(s, 1, 0)
                    split_weights(s, 1, 0)
                if has_ffn(n) and n % DPB == 1:
                    dve.wait_ge(w2_hi_ready, s.at(lambda n: n // DPB))
                    nc.vector.tensor_tensor(w2_lo[:, 4:8, :], (w2raw if n < ND else w2raw_end)[:, 4:8, :], w2_hi[:, 4:8, :].bitcast(F32), ALU.subtract)\
                      .then_inc(w2_split, 1)
                if has_attn(n):
                    normalise(s, 0)
                if n + 2 < ND:
                    measure_first(s)
                if has_attn(n):
                    split_attn(s, 0)
                    mask_weights(s, 1, 1)
                if has_route(n):
                    route(s)
                if has_attn(n):
                    split_weights(s, 1, 1)
                    residual(s, 0)
                if n + 2 < ND:
                    apply_first(s)
                if has_ffn(n):
                    finish(s, 0)
                if has_front(n):
                    add_value_bias(s)
                if has_attn(n):
                    normalise(s, 1)
                if has_route(n):
                    dve.wait_ge(w1_hi_ready, s.at(lambda n: 2 * (n // DPB)))
                    nc.vector.tensor_tensor(w1_lo[:, 1, :, :], w1raw[:, 1, :].rearrange("p (q f) -> p f q", f=FC),
                                            w1_hi[:, 1, :, :].bitcast(F32), ALU.subtract).then_inc(w1_split, 1)
                if has_ffn(n):
                    finish(s, 1)
                if has_attn(n):
                    split_attn(s, 1)
                    residual(s, 1)

            run(dve, step)

        @block.tensor
        def _(pe):
            def transpose_weight(f):
                if f == 0:
                    pe.wait_ge(s_wqkv, 16)
                if f == 3:
                    pe.wait_ge(s_wout, 16)
                if f >= 2:
                    pe.wait_ge(setup_freed, f - 1)
                raw = wqkv_raw[:, 2 * f:2 * f + 2, :] if f < 3 else wout_raw
                for j in range(CJ):
                    for o in range(CJ):
                        last = nc.tensor.transpose(dve_bank[f % 2][:, (2 * j + o) * P:(2 * j + o + 1) * P],
                                                   raw[:, o, j * P:(j + 1) * P], ident[:, :])
                last.then_inc(setup_filled, 1)

            def wmod_cols(j, first, width):
                if first < 1024:
                    return wmod_a[:, j, first:first + width]
                return wmod_b[:, j, first - 1024:first - 1024 + width]

            def modulation(norm):
                for q in range(2):
                    for oj in range(CJ):
                        at = (q * CJ + oj) * B
                        for j in range(CJ):
                            last = nc.tensor.matmul(ctx_bank[norm][:, at:at + B],
                                                    wmod_cols(j, (3 * norm + q) * C + oj * P, P), scT[:, j, :],
                                                    start=j == 0, stop=j == CJ - 1)
                last.then_inc(mod_filled, 1)

            def setup_rest():
                transpose_weight(3)
                pe.wait_ge(s_wmod_rest, 32)
                modulation(1)

            def gates():
                for g, part in enumerate((2, 5)):
                    for j in range(CJ):
                        last = nc.tensor.matmul(kv_bank[0:B, g * C:(g + 1) * C], scT[:, j, :], wmod_cols(j, part * C, C),
                                                start=j == 0, stop=j == CJ - 1)
                last.then_inc(mod_filled, 1)

            def product(dst, w, y, start, stop):
                (w_hi, w_lo), (y_hi, y_lo) = w, y
                nc.tensor.matmul(dst, w_hi, y_hi, start=start, stop=False)
                nc.tensor.matmul(dst, w_hi, y_lo, start=False, stop=False)
                return nc.tensor.matmul(dst, w_lo, y_hi, start=False, stop=stop)

            def act_fill(s, name):
                at = fill(act_fills, name)
                if at(s.n) >= 2:
                    pe.wait_ge(act_freed, s.at(lambda n: at(n) - 1))
                return act_bank[at(s.n) % 2]

            def dve_fill(s, name):
                at = fill(dve_fills, name)
                if at(s.n) >= 3:
                    pe.wait_ge(dve_freed, s.at(lambda n: at(n) - 2))
                return dve_bank[at(s.n) % 3]

            def transpose_norm(s, name, src):
                ps = act_fill(s, name)
                for j in range(CJ):
                    for i in range(2):
                        last = nc.tensor.transpose(ps[:, j * DUO + i * P:j * DUO + (i + 1) * P],
                                                   src[:, i, j * P:(j + 1) * P], ident[:, :])
                last.then_inc(act_filled, 1)

            def project_qk(s, w):
                pe.wait_ge(hT_split, s.at(lambda n: n + 2))
                ps = act_fill(s, f"qk{w}")
                for g in range(CJ):
                    cols = slice((2 * w + g) * P, (2 * w + g + 1) * P)
                    for j in range(CJ):
                        last = product(ps[:, g * DUO:(g + 1) * DUO],
                                       (wqkvT_hi[:, j, cols], wqkvT_lo[:, j, cols]),
                                       (hT_hi[:, j, :], hT_lo[:, j, :]), j == 0, j == CJ - 1)
                last.then_inc(act_filled, 1)

            def project_v(s):
                ps = dve_fill(s, "v")
                for i in range(2):
                    toks = slice(i * P, (i + 1) * P)
                    for j in range(CJ):
                        last = product(ps[:, i * C:(i + 1) * C], (hT_hi[:, j, toks], hT_lo[:, j, toks]),
                                       (wqkvT_hi[:, j, 2 * C:3 * C], wqkvT_lo[:, j, 2 * C:3 * C]), j == 0, j == CJ - 1)
                last.then_inc(dve_filled, 1)

            def features(s, w, tiles):
                if tiles[0] == 0:
                    pe.wait_ge(qk_split, s.at(lambda n: 2 * (n + 1) + 2 - w))
                for j in tiles:
                    ps = act_fill(s, f"feat{w}{j}")
                    rows = slice(32 * j, 32 * j + 32)
                    for g in range(CJ):
                        proj_parts = (pbd_hi[rows, g, :], pbd_lo[rows, g, :])
                        if s.n < DPB:
                            rows = slice(0, P)
                            proj_parts = [part[:, 4 * g + j, :] for part in padded]
                        last = product(ps[:, g * DUO:(g + 1) * DUO], proj_parts,
                                       (qkT_hi[rows, w, g, :], qkT_lo[rows, w, g, :]), True, True)
                    last.then_inc(act_filled, 1)

            def weights(s, i, r):
                fq, fk = feat
                toks = slice(i * P, (i + 1) * P)
                banks = [dve_fill(s, f"aw{i}{2 * r + a}") for a in range(2)]
                for j in range(4):
                    last = []
                    for a in range(2):
                        rows = slice(a * M, (a + 1) * M)
                        last.append(nc.tensor.matmul(banks[a][:, j * P:(j + 1) * P], fk[rows, 4 * r + j, toks],
                                                     fq[rows, 4 * r + j, toks], start=True, stop=True))
                for a in range(2):
                    last[a].then_inc(dve_filled, 1)

            def transpose_keys(s, i, half):
                if is_last(s.n, i):
                    return
                ps = act_fill(s, f"kp{i}{half}")
                for j in range(4):
                    last = nc.tensor.transpose(ps[:, j * P:(j + 1) * P], feat[1][:, 4 * half + j, i * P:(i + 1) * P],
                                               ident[:, :])
                last.then_inc(act_filled, 1)

            def context(s, i, b):
                toks = slice(i * P, (i + 1) * P)
                first_chunk = s.n % DPB == 0 and i == 0
                va = v_parts[:, s.n % 2, i, :, :, :].rearrange("p h q w -> p h (q w)")
                if i == 0 and b == 0:
                    pe.wait_ge(v_split, s.at(lambda n: n + 1))
                if b == 0 and (s.n > 0 or i > 0):
                    pe.wait_ge(attn_ready, s.at(lambda n: 2 * n + i))
                if has_route(s.n) and i == 1 and b == 0:
                    pe.wait_ge(route_read, s.at(lambda n: n // DPB))
                if b == 0 and not first_chunk:
                    pe.wait_ge(kv_ready, s.at(lambda n: chunks_with_state(n, i - 1)))
                pe.wait_ge(aw_split, s.at(lambda n: 2 * (2 * n + i) + b + 1))
                for pair in range(4 * b, 4 * b + 4):
                    ps = ctx_bank[b][:, 0:H // 2 * PARTS * VW].rearrange("p (h q w) -> p h q w", q=PARTS, w=VW)
                    at = 2 * (pair % 4)
                    if not first_chunk:
                        nc.tensor.matmul(ps[:, at:at + 2, 0, :], feat[0][:, pair, toks],
                                         kvbd[:, pair, :].rearrange("p (a w) -> p a w", a=2),
                                         start=at == 0, stop=False, skip_group_check=True)
                    for a in range(2):
                        for q in range(PARTS):
                            last = nc.tensor.matmul(ps[:, at + a, :, :].rearrange("p q w -> p (q w)"),
                                                    aw[q][:, pair // 4, a, pair % 4, :], va[:, 2 * pair + a, :],
                                                    start=first_chunk and at + a + q == 0, stop=at + a + q == 7 + PARTS - 1,
                                                    skip_group_check=True)
                last.then_inc(ctx_filled, 1)

            def state(s, i):
                if is_last(s.n, i):
                    return
                first_chunk = s.n % DPB == 0 and i == 0
                if s.n > 0 or i > 0:
                    pe.wait_ge(kv_ready, s.at(lambda n: chunks_with_state(n, i) - 1))
                pe.wait_ge(act_freed, s.at(lambda n: fill(act_fills, f"kp{i}1")(n) + 1))
                va = vaug[:, s.n % 2, i, :, :].rearrange("p h w -> p (h w)")
                for pair in range(NPAIR):
                    cols = slice(pair * 2 * VW, (pair + 1) * 2 * VW)
                    last = nc.tensor.matmul(kv_bank[:, cols], kp[:, pair, :], va[:, cols],
                                            start=first_chunk and pair == 0, stop=pair == NPAIR - 1,
                                            skip_group_check=True)
                last.then_inc(kv_filled, 1)

            def transpose_attn(s, i):
                ps = dve_fill(s, f"aT{i}")
                pe.wait_ge(attn_ready, s.at(lambda n: 2 * n + i + 1))
                for j in range(CJ):
                    last = nc.tensor.transpose(ps[:, j * P:(j + 1) * P], attn[:, j * P:(j + 1) * P], ident[:, :])
                last.then_inc(dve_filled, 1)

            def project_out(s, i):
                ps = dve_fill(s, f"o{i}")
                pe.wait_ge(dve_freed, s.at(lambda n: fill(dve_fills, f"aT{i}")(n) + 1))
                for j in range(CJ):
                    last = product(ps[:, 0:C], (aT_hi[:, j, :], aT_lo[:, j, :]), (woT_hi[:, j, :], woT_lo[:, j, :]),
                                   j == 0, j == CJ - 1)
                last.then_inc(dve_filled, 1)

            def route(s):
                pe.wait_ge(attn_ready, s.at(lambda n: 2 * n + 1) if has_attn(s.n) else 2 * s.n)
                pe.wait_ge(act_freed, s.at(lambda n: fill(act_fills, "x2T")(n) + 1))
                parts = [(j, d) for j in range(CJ) for d in range(DPB)]
                for at, (j, d) in enumerate(parts):
                    last = nc.tensor.matmul(ctx_bank[0][0:1, 0:E], hsum[:, j, d:d + 1], wr_sb[:, j, :],
                                            start=at == 0, stop=at == len(parts) - 1)
                last.then_inc(route_filled, 1)

            def up(s, q):
                if q == 0:
                    pe.wait_ge(hF_split, s.at(lambda n: n - FFN_LAG + 1))
                    if s.n % DPB == 1:
                        pe.wait_ge(w1_split, s.at(lambda n: 2 * (n // DPB)))
                ps = act_fill(s, f"up{q}")
                slot = (s.n - FFN_LAG) % DPB
                for a in range(2):
                    for j in range(CJ):
                        last = product(ps[:, a * DUO:(a + 1) * DUO], (w1_hi[:, j, 2 * q + a, :], w1_lo[:, j, 2 * q + a, :]),
                                       (hF_hi[:, slot, j, :], hF_lo[:, slot, j, :]), j == 0, j == CJ - 1)
                last.then_inc(act_filled, 1)

            def down(s, i, half):
                if i == 0:
                    pe.wait_ge(h1_split, s.at(lambda n: 4 * (n - FFN_LAG) + 2 * half + 2))
                    if s.n % DPB == 1 and half == 0:
                        pe.wait_ge(w2_split, s.at(lambda n: 2 * (n // DPB)))
                if half == 0:
                    down_bank[i] = dve_fill(s, f"down{i}")
                toks = slice(i * P, (i + 1) * P)
                for f in range(half * FC // 2, (half + 1) * FC // 2):
                    last = product(down_bank[i][:, 0:C], (h1_hi[:, f, toks], h1_lo[:, f, toks]),
                                   (w2_hi[:, f, :], w2_lo[:, f, :]), f == 0, f == FC - 1)
                if half == 1:
                    last.then_inc(dve_filled, 1)

            down_bank = [None, None]

            def step(s):
                n = s.n
                front, attn, ffn = has_front(n), has_attn(n), has_ffn(n)
                if front:
                    pe.wait_ge(xn_ready, s.at(lambda n: 2 * (n + 2)))
                    transpose_norm(s, "xT", xn)
                if n == -1:
                    setup_rest()
                    pe.wait_ge(pbd_ready, 6)
                    pe.wait_ge(setup_freed, 4)
                    pe.wait_ge(padded_ready, 10)
                if attn:
                    pe.wait_ge(act_freed, s.at(lambda n: fill(act_fills, "feat03")(n - 1) + 1))
                    transpose_keys(s, 0, 0)
                    weights(s, 0, 0)
                if ffn:
                    up(s, 0)
                if attn:
                    weights(s, 0, 1)
                    transpose_keys(s, 0, 1)
                if ffn:
                    up(s, 1)
                if front:
                    project_qk(s, 1)
                if n == -1:
                    gates()
                if attn:
                    weights(s, 1, 0)
                    context(s, 0, 0)
                if ffn:
                    up(s, 2)
                if attn:
                    context(s, 0, 1)
                    state(s, 0)
                if ffn:
                    up(s, 3)
                if has_ln2(n):
                    pe.wait_ge(xn2_ready, s.at(lambda n: 2 * n))
                    transpose_norm(s, "x2T", xn2)
                if attn:
                    transpose_attn(s, 0)
                    weights(s, 1, 1)
                    transpose_keys(s, 1, 0)
                if has_route(n):
                    route(s)
                if ffn and not attn:
                    for half in range(2):
                        down(s, 0, half)
                        down(s, 1, half)
                    return
                if ffn:
                    down(s, 0, 0)
                if attn:
                    transpose_keys(s, 1, 1)
                    project_out(s, 0)
                if front:
                    features(s, 1, (0, 1))
                if ffn:
                    down(s, 0, 1)
                if front:
                    project_qk(s, 0)
                    features(s, 1, (2,))
                    project_v(s)
                    features(s, 1, (3,))
                if attn:
                    context(s, 1, 0)
                if ffn:
                    down(s, 1, 0)
                if attn:
                    context(s, 1, 1)
                if front:
                    features(s, 0, (0, 1))
                if ffn:
                    down(s, 1, 1)
                if attn:
                    transpose_attn(s, 1)
                if front:
                    features(s, 0, (2, 3))
                if attn:
                    state(s, 1)
                    project_out(s, 1)

            pe.wait_ge(consts_ready, 2)
            for f in range(3):
                transpose_weight(f)
            pe.wait_ge(silu_ready, 1)
            pe.wait_ge(s_wmod_first, 16)
            modulation(0)
            run(pe, step)


_INS = ["L0_attn_x", "L0_attn_Wqkv", "L0_attn_bqkv", "L0_attn_Wout", "L0_attn_bout", "L0_attn_proj", "L0_ffn_Wr",
        "L0_ffn_br", "L0_ffn_W1", "L0_ffn_b1", "L0_ffn_W2", "L0_ffn_b2", "L0_c", "L0_wmod"]


def kernel(**inputs):
    import numpy as _np
    import concourse.bacc as _bacc
    from concourse.bass_utils import run_bass_kernel_spmd as _run

    nc = _bacc.Bacc("TRN2", target_bir_lowering=False, num_devices=1)
    arrays, args = {}, []
    for name in _INS:
        a = _np.ascontiguousarray(inputs[name])
        arrays[f"in_{name}"] = a
        args.append(nc.dram_tensor(f"in_{name}", a.shape, mybir.dt.from_np(a.dtype), kind="ExternalInput").ap())
    args.append(nc.dram_tensor("out_0", (B, T, C), F32, kind="ExternalOutput").ap())
    program(nc, *args)
    return _run(nc, [arrays], core_ids=[0]).results[0]["out_0"]
```
